# Optimizing a Trainium2 kernel written in Bass

```python
import numpy as np
import jax
import jax.numpy as jnp

def _softmax(x, axis=-1):
    return jax.nn.softmax(x, axis=axis)

def _gelu(x):
    return jax.nn.gelu(x, approximate=True)

def _silu(x):
    return jax.nn.silu(x)

def _sigmoid(x):
    return jax.nn.sigmoid(x)

def _layernorm(x, axis=-1, eps=1e-05):
    m = jnp.mean(x, axis=axis, keepdims=True)
    v = jnp.var(x, axis=axis, keepdims=True)
    return (x - m) / jnp.sqrt(v + eps)

def _scatter_add(tgt, idx, src, axis=0):
    return tgt.at[idx].add(src)

def _segment_sum(src, seg, n):
    return jax.ops.segment_sum(src, seg, n)
kernel_name = 'mk_xattn_ffn_d1_seqx_r2_a729a8'

def setup_inputs(seed: int=0):
    np.random.seed(seed)
    _w = jnp.asarray

    def _rec_inputs():
        import jax
        import jax.numpy as jnp
        _rk = jax.random.key(seed)
        x = 7.22e-05 + 1 * jax.random.normal(jax.random.fold_in(_rk, 1), (8, 1024, 512), jnp.float32)
        _lenS = 1024 - jax.random.randint(jax.random.fold_in(_rk, 7), (8,), 0, max(1, 1024 // 4) + 1, jnp.int32)
        _lenS2 = 64 - jax.random.randint(jax.random.fold_in(_rk, 8), (8,), 0, max(1, 64 // 4) + 1, jnp.int32)
        _ctx_768P = jax.random.normal(jax.random.fold_in(_rk, 11), (8, 16, 384), jnp.float32)
        _ctx_768c = jax.random.dirichlet(jax.random.fold_in(_rk, 511), 0.3 * jnp.ones((16,), jnp.float32), (8, 64))
        _ctx_768t = jnp.einsum('bsk,bkd->bsd', _ctx_768c, _ctx_768P)
        _ctx_768t = _ctx_768t * jax.lax.rsqrt(jnp.mean(jnp.square(_ctx_768t)) + 1e-12) * 0.953939
        ctx_768 = -0.000191848 + 0.999787 * (_ctx_768t + 0.3 * jax.random.normal(jax.random.fold_in(_rk, 611), (8, 64, 384), jnp.float32))
        return (x, ctx_768)
    x, ctx_768 = _rec_inputs()

    def _L0_xattn_setup():
        import jax, jax.numpy as jnp
        import numpy as np
        NUM_HEADS = 16
        CLAMP = 10000.0
        key = jax.random.key(seed)
        ks = jax.random.split(key, 8)
        B, Nq, Nkv, Cq, Ckv = (4, 1024, 1024, 512, 384)
        s_q = 1.0 / np.sqrt(Cq)
        s_kv = 1.0 / np.sqrt(Ckv)
        return {'query': jax.random.normal(ks[0], (B, Nq, Cq), jnp.float32), 'key_value': jax.random.normal(ks[1], (B, Nkv, Ckv), jnp.float32), 'Wq': jax.random.normal(ks[2], (Cq, Cq), jnp.float32) * s_q, 'bq': jnp.zeros((Cq,), jnp.float32), 'Wk': jax.random.normal(ks[3], (Ckv, Cq), jnp.float32) * s_kv, 'bk': jnp.zeros((Cq,), jnp.float32), 'Wv': jax.random.normal(ks[4], (Ckv, Cq), jnp.float32) * s_kv, 'bv': jnp.zeros((Cq,), jnp.float32), 'Wo': jax.random.normal(ks[5], (Cq, Cq), jnp.float32) * s_q, 'bo': jnp.zeros((Cq,), jnp.float32)}
    _L0_xattn_all = _L0_xattn_setup()
    _L0_xattn_in = {k: v for k, v in _L0_xattn_all.items() if k in ('Wq', 'bq', 'Wk', 'bk', 'Wv', 'bv', 'Wo', 'bo')}
    del _L0_xattn_all

    def _L0_ffn_setup():
        import jax, jax.numpy as jnp
        import numpy as np
        B, S, D_MODEL, D_FF = (4, 1024, 512, 2048)

        def _quantum_transform(hidden, theta, w_real, w_imag):
            imag = w_imag * jnp.sin(theta + hidden * 0.1)
            quantum_phase = jnp.cos(theta) * w_real + jnp.sin(theta) * w_imag
            return hidden + quantum_phase * imag * 0.1
        key = jax.random.key(seed)
        ks = jax.random.split(key, 8)
        return {'x': jax.random.normal(ks[0], (B, S, D_MODEL), dtype=jnp.float32), 'W1': jax.random.normal(ks[1], (D_MODEL, D_FF), dtype=jnp.float32) * (1.0 / np.sqrt(D_MODEL)), 'b1': jnp.zeros((D_FF,), dtype=jnp.float32), 'quantum_phases': jax.random.normal(ks[2], (D_FF,), dtype=jnp.float32) * (2.0 * np.pi), 'quantum_weights_real': jax.random.normal(ks[3], (D_FF,), dtype=jnp.float32) * 0.1, 'quantum_weights_imag': jax.random.normal(ks[4], (D_FF,), dtype=jnp.float32) * 0.1, 'W2': jax.random.normal(ks[5], (D_FF, D_MODEL), dtype=jnp.float32) * (1.0 / np.sqrt(D_FF)), 'b2': jnp.zeros((D_MODEL,), dtype=jnp.float32)}
    _L0_ffn_all = _L0_ffn_setup()
    _L0_ffn_in = {k: v for k, v in _L0_ffn_all.items() if k in ('W1', 'b1', 'quantum_phases', 'quantum_weights_real', 'quantum_weights_imag', 'W2', 'b2')}
    del _L0_ffn_all
    return {'x': x, 'ctx_768': ctx_768, 'L0_xattn_Wq': _L0_xattn_in['Wq'], 'L0_xattn_bq': _L0_xattn_in['bq'], 'L0_xattn_Wk': _L0_xattn_in['Wk'], 'L0_xattn_bk': _L0_xattn_in['bk'], 'L0_xattn_Wv': _L0_xattn_in['Wv'], 'L0_xattn_bv': _L0_xattn_in['bv'], 'L0_xattn_Wo': _L0_xattn_in['Wo'], 'L0_xattn_bo': _L0_xattn_in['bo'], 'L0_ffn_W1': _L0_ffn_in['W1'], 'L0_ffn_b1': _L0_ffn_in['b1'], 'L0_ffn_quantum_phases': _L0_ffn_in['quantum_phases'], 'L0_ffn_quantum_weights_real': _L0_ffn_in['quantum_weights_real'], 'L0_ffn_quantum_weights_imag': _L0_ffn_in['quantum_weights_imag'], 'L0_ffn_W2': _L0_ffn_in['W2'], 'L0_ffn_b2': _L0_ffn_in['b2']}

def reference(x, ctx_768, L0_xattn_Wq, L0_xattn_bq, L0_xattn_Wk, L0_xattn_bk, L0_xattn_Wv, L0_xattn_bv, L0_xattn_Wo, L0_xattn_bo, L0_ffn_W1, L0_ffn_b1, L0_ffn_quantum_phases, L0_ffn_quantum_weights_real, L0_ffn_quantum_weights_imag, L0_ffn_W2, L0_ffn_b2):
    import jax
    import jax.numpy as jnp

    def _L0_xattn_ref(query, key_value, Wq, bq, Wk, bk, Wv, bv, Wo, bo):
        import jax, jax.numpy as jnp
        import numpy as np
        NUM_HEADS = 16
        CLAMP = 10000.0
        B, Nq, Cq = query.shape
        Nkv = key_value.shape[1]
        H = NUM_HEADS
        D = Cq // H
        scale = D ** (-0.5)
        q = (query @ Wq + bq).reshape(B, Nq, H, D).transpose(0, 2, 1, 3)
        k = (key_value @ Wk + bk).reshape(B, Nkv, H, D).transpose(0, 2, 1, 3)
        v = (key_value @ Wv + bv).reshape(B, Nkv, H, D).transpose(0, 2, 1, 3)
        attn = jnp.einsum('bhqd,bhkd->bhqk', q, k) * scale
        attn = jnp.clip(attn, -CLAMP, CLAMP)
        attn = jax.nn.softmax(attn, axis=-1)
        attn = jnp.where(jnp.any(jnp.isnan(attn)), jnp.asarray(1.0 / Nkv, attn.dtype), attn)
        x = jnp.einsum('bhqk,bhkd->bqhd', attn, v).reshape(B, Nq, Cq)
        return x @ Wo + bo

    def _L0_ffn_ref(x, W1, b1, quantum_phases, quantum_weights_real, quantum_weights_imag, W2, b2):
        import jax, jax.numpy as jnp
        import numpy as np
        B, S, D_MODEL, D_FF = (4, 1024, 512, 2048)

        def _quantum_transform(hidden, theta, w_real, w_imag):
            imag = w_imag * jnp.sin(theta + hidden * 0.1)
            quantum_phase = jnp.cos(theta) * w_real + jnp.sin(theta) * w_imag
            return hidden + quantum_phase * imag * 0.1
        hidden = jnp.einsum('bsd,df->bsf', x, W1) + b1
        q = _quantum_transform(hidden, quantum_phases, quantum_weights_real, quantum_weights_imag)
        act = jax.nn.relu(q)
        return jnp.einsum('bsf,fd->bsd', act, W2) + b2
    x = x + _L0_xattn_ref(_layernorm(x, axis=-1), ctx_768, L0_xattn_Wq, L0_xattn_bq, L0_xattn_Wk, L0_xattn_bk, L0_xattn_Wv, L0_xattn_bv, L0_xattn_Wo, L0_xattn_bo)
    x = x + _L0_ffn_ref(_layernorm(x, axis=-1), L0_ffn_W1, L0_ffn_b1, L0_ffn_quantum_phases, L0_ffn_quantum_weights_real, L0_ffn_quantum_weights_imag, L0_ffn_W2, L0_ffn_b2)
    return x

_drawn_inputs = setup_inputs


def setup_inputs(seed=0):
    import zlib

    import numpy as np

    out = dict(_drawn_inputs(seed))
    spreads = {'L0_xattn_bq': (0.0, 0.385),
     'L0_xattn_bk': (0.0, 2.0),
     'L0_xattn_bv': (0.0, 0.1),
     'L0_xattn_bo': (0.0, 0.1),
     'L0_ffn_b1': (0.0, 0.1),
     'L0_ffn_b2': (0.0, 0.1)}
    factors = {'L0_ffn_quantum_phases': 8.0,
     'L0_ffn_quantum_weights_real': 42.361,
     'L0_ffn_quantum_weights_imag': 8.0}
    for name, (base, spread) in spreads.items():
        noise = np.random.default_rng([zlib.crc32(name.encode()), seed]).standard_normal(out[name].shape)
        drawn = base * np.exp(spread * noise) if base else spread * noise
        out[name] = jnp.asarray(drawn.astype(out[name].dtype))
    for name, factor in factors.items():
        out[name] = (out[name] * factor).astype(out[name].dtype)
    return out
```

```python
from contextlib import ExitStack
import math

import numpy as np

import concourse.bass as bass
from concourse import mybir

F32 = mybir.dt.float32
F32R = mybir.dt.float32r
I32 = mybir.dt.int32
ALU = mybir.AluOpType
ACT = mybir.ActivationFunctionType
AX_X = mybir.AxisListType.X

P = 128
BANKS, BANK = 8, 512
B, N, C = 8, 1024, 512
HEADS, KEYS, CK = 16, 64, 384
FF = 2048
D = C // HEADS
SCALE = float(D) ** -0.5
CLAMP = 10000.0
EPS = 1e-5

TOK = 512
TILES = B * N // TOK
TPB = N // TOK
NB = TOK // P
KC = C // P
KK = CK // P
HG = P // D
GROUPS = TILES * KC
GB = TPB * KC
SG = HG * KEYS
PAIRS = HG // 2
FC = FF // P
HALF1 = FC // 2

ROUND = 1.5 * 2.0 ** 23
TWO_PI = 2.0 * math.pi
SIN_SCALE = 6.283185
PI_A = 6.28125
PI_B = float(np.float32(np.round((TWO_PI - PI_A) * 2.0 ** 20) / 2.0 ** 20))
PI_C = TWO_PI - PI_A - PI_B

LAG_A = 2
LAG_B = 3
SCORE_BUFS = 3
STAGE = 4
STAGE_B = 2
ACTS = LAG_B + 1
XBUFS_A, XBUFS_B = 3, 2
LN_AT = 5
CONSTS = 15
PAR_REDUCED = 13
VN_BANK, VM_BANK, U_BANK = 0, 1, 0


class Waits:

    def __init__(self, engine):
        self.engine, self.seen = engine, {}

    def __call__(self, sem, value):
        if value > self.seen.get(id(sem), 0):
            self.engine.wait_ge(sem, value)
            self.seen[id(sem)] = value


def plan_phase_a():
    order = [("xt", k) for k in range(KC)] + [("q", 0)]
    for i in range(GROUPS + LAG_A):
        late = i - LAG_A
        if i < GROUPS:
            order.append(("s", i))
        if late >= 0:
            order += [("pt", late * PAIRS + j) for j in range(PAIRS)]
        if i + 1 < GROUPS:
            order.append(("q", i + 1))
            if i % KC == KC - 2 and i + 2 < GROUPS:
                tile = i // KC + 1
                order += [("xt", tile * KC + k) for k in range(KC)]
        if late >= 0:
            order.append(("o", late))
            if late % KC == KC - 1:
                order += [("y", late // KC * NB + blk) for blk in range(NB)]
    return order


def plan_phase_b():
    order = [("xt", (TILES * KC) + k) for k in range(KC)]
    for t in range(TILES):
        for f in range(FC):
            j = t * FC + f
            order.append(("h", j))
            if f >= LAG_B:
                last = f == FC - 1
                if last and t + 1 < TILES:
                    order += [("xt", (TILES + t + 1) * KC + k) for k in range(KC)]
                order.append(("f", j - LAG_B))
                if last:
                    order.append(("f", j - LAG_B + 1))
            elif t > 0 and f < LAG_B - 1:
                order.append(("f", j - LAG_B + 1))
    order += [("f", TILES * FC - LAG_B + 1 + n) for n in range(LAG_B - 1)]
    return order


def xattn_ffn(nc, x, ctx_768, wq, bq, wk, bk, wv, bv, wo, bo_row_in, bo, w1, b1, phases, w_real, w_imag, w2, b2,
              out, x1_dram, v_dram, u_dram):
    x_rows = x.rearrange("b (t n p) c -> (b t) p n c", n=NB, p=P)
    x1_rows = x1_dram.rearrange("(t n p) c -> t p n c", n=NB, p=P)
    out_rows = out.rearrange("b (t n p) c -> (b t) p n c", n=NB, p=P)

    stack = ExitStack()
    with stack:
        def sem(name):
            return stack.enter_context(nc.semaphore(name))

        def sems(name, n):
            return [sem(f"{name}{i}") for i in range(n)]

        def sbuf(where, name, shape, dt=F32):
            return where.enter_context(nc.sbuf_tensor(name, shape, dt))

        ident = sbuf(stack, "ident", [P, P])
        ones = sbuf(stack, "ones", [P, 1])
        x_sb = [sbuf(stack, f"x_sb{i}", [P, NB, C]) for i in range(XBUFS_B)]
        xn = sbuf(stack, "xn", [P, NB, C])
        xt_hi = sbuf(stack, "xt_hi", [P, KC, TOK], F32R)
        xt_lo = sbuf(stack, "xt_lo", [P, KC, TOK], F32R)
        stats = sbuf(stack, "stats", [P, 2, NB, 6])
        mv = sbuf(stack, "mv", [P, 2, NB, 2])
        var_eps = sbuf(stack, "var_eps", [P, 2, NB])
        rstd = sbuf(stack, "rstd", [P, 2, NB])
        minus_half = sbuf(stack, "minus_half", [P, NB])
        bq_sb = sbuf(stack, "bq_sb", [P, KC])
        bk_sb = sbuf(stack, "bk_sb", [P, KC])
        par = sbuf(stack, "par", [P, 4, FC])
        red = sbuf(stack, "red", [P, 8, FC])
        u_shift = sbuf(stack, "u_shift", [P, FC])
        gain = sbuf(stack, "gain", [P, FC])
        squares = sbuf(stack, "squares", [P, 2 * GROUPS])
        not_nan = sbuf(stack, "not_nan", [P, 2 * GROUPS])
        row_ok = sbuf(stack, "row_ok", [P, 1])
        ok_count = sbuf(stack, "ok_count", [1, 1], I32)

        start = ExitStack()
        wk_sb = sbuf(start, "wk_sb", [P, KK, C])
        wv_sb = sbuf(start, "wv_sb", [P, KK, C])
        ctx_sb = sbuf(start, "ctx_sb", [P, B // 2, CK])
        ctxt = sbuf(start, "ctxt", [P, KK, B * KEYS])
        v_sb = sbuf(start, "v_sb", [P, 1, C])
        bv_row = sbuf(start, "bv_row", [P, C])
        start.close()
        w1a_hi = sbuf(stack, "w1a_hi", [P, HALF1, KC, P], F32R)
        w1a_lo = sbuf(stack, "w1a_lo", [P, HALF1, KC, P], F32R)

        pa = ExitStack()
        x_sb_a = x_sb + [sbuf(pa, f"x_sb{i}", [P, NB, C]) for i in range(XBUFS_B, XBUFS_A)]
        wq_hi = sbuf(pa, "wq_hi", [P, KC, C], F32R)
        wq_lo = sbuf(pa, "wq_lo", [P, KC, C], F32R)
        wo_hi = sbuf(pa, "wo_hi", [P, KC, C], F32R)
        wo_lo = sbuf(pa, "wo_lo", [P, KC, C], F32R)
        stage = sbuf(pa, "stage", [P, STAGE, C])
        kt = sbuf(pa, "kt", [P, KC, B * KEYS])
        k_masked = sbuf(pa, "k_masked", [P, HG, KEYS])
        kbd_hi = sbuf(pa, "kbd_hi", [P, KC, SG], F32R)
        kbd_lo = sbuf(pa, "kbd_lo", [P, KC, SG], F32R)
        v_in = sbuf(pa, "v_in", [P, 2, C])
        v_masked = sbuf(pa, "v_masked", [P, PAIRS, P])
        vbd_hi = sbuf(pa, "vbd_hi", [P, KC, PAIRS, P], F32R)
        vbd_lo = sbuf(pa, "vbd_lo", [P, KC, PAIRS, P], F32R)
        mask_k = sbuf(pa, "mask_k", [P, HG])
        mask_v = sbuf(pa, "mask_v", [P, PAIRS, P])
        q_hi = sbuf(pa, "q_hi", [P, 2, TOK], F32R)
        q_lo = sbuf(pa, "q_lo", [P, 2, TOK], F32R)
        prob = sbuf(pa, "prob", [P, SCORE_BUFS, NB * HG, KEYS])
        square = sbuf(pa, "square", [P, 2, BANK], mybir.dt.bfloat16)
        top = sbuf(pa, "top", [P, 2, NB * HG])
        total = sbuf(pa, "total", [P, 2, NB * HG])
        inv = sbuf(pa, "inv", [P, 2, NB * HG])
        pt_hi = sbuf(pa, "pt_hi", [P, PAIRS, TOK], F32R)
        pt_lo = sbuf(pa, "pt_lo", [P, PAIRS, TOK], F32R)
        o_hi = sbuf(pa, "o_hi", [P, KC, TOK], F32R)
        o_lo = sbuf(pa, "o_lo", [P, KC, TOK], F32R)
        bo_row = sbuf(pa, "bo_row", [P, C])
        v_mean = sbuf(pa, "v_mean", [P, KC, B])
        vm_hi = sbuf(pa, "vm_hi", [P, KC, B], F32R)
        vm_lo = sbuf(pa, "vm_lo", [P, KC, B], F32R)
        pick = sbuf(pa, "pick", [P, 2])
        u_sb = sbuf(pa, "u_sb", [P, KC, B])
        bo_col = sbuf(pa, "bo_col", [P, KC])
        pa.close()

        pb = ExitStack()
        w1b_hi = sbuf(pb, "w1b_hi", [P, FC - HALF1, KC, P], F32R)
        w1b_lo = sbuf(pb, "w1b_lo", [P, FC - HALF1, KC, P], F32R)
        w2_hi = sbuf(pb, "w2_hi", [P, FC, C], F32R)
        w2_lo = sbuf(pb, "w2_lo", [P, FC, C], F32R)
        stage_b = sbuf(pb, "stage_b", [P, STAGE_B, C])
        turns = sbuf(pb, "turns", [P, 2, TOK])
        frac = sbuf(pb, "frac", [P, 2, TOK])
        hid = sbuf(pb, "hid", [P, 2, TOK])
        act_hi = sbuf(pb, "act_hi", [P, ACTS, TOK], F32R)
        act_lo = sbuf(pb, "act_lo", [P, ACTS, TOK], F32R)
        b2_row = sbuf(pb, "b2_row", [P, C])
        pb.close()

        psum = stack.enter_context(nc.psum_tensor("psum", [P, BANKS, BANK], F32))

        order_a, order_b = plan_phase_a(), plan_phase_b()
        S_BANKS = NB * SG // BANK
        RING_A, RING_B = list(range(S_BANKS, BANKS)), list(range(NB))
        Y_BANK = NB
        bank_of, before = {}, {}

        def go_round(items, ring, kinds):
            held = {}
            for n, item in enumerate(it for it in items if it[0] in kinds):
                bank_of[item] = ring[n % len(ring)]
                before[item] = held.get(bank_of[item])
                held[bank_of[item]] = item

        go_round(order_a, RING_A, ("xt", "q", "pt", "o", "y"))
        go_round(order_b, RING_B, ("xt", "h"))

        def bank(item):
            return psum[:, bank_of[item], :]

        const_ready = sem("const_ready")
        ctx_in, kw_in, vw_in, bias_in, par_in, b2_in = (sem(n) for n in (
            "ctx_in", "kw_in", "vw_in", "bias_in", "par_in", "b2_in"))
        ctxt_psum, ctxt_done = sem("ctxt_psum"), sem("ctxt_done")
        kt_psum, kt_done = sem("kt_psum"), sem("kt_done")
        vn_psum, vn_done, vn_stored = sem("vn_psum"), sem("vn_done"), sem("vn_stored")
        vm_pair, bq_scaled = sem("vm_pair"), sem("bq_scaled")
        vm_psum, vm_done, vm_hi_done, vm_lo_done = (sem(n) for n in ("vm_psum", "vm_done", "vm_hi_done", "vm_lo_done"))
        u_psum, u_done, u_stored = sem("u_psum"), sem("u_done"), sem("u_stored")
        par_step, par_sin, par_done = sem("par_step"), sem("par_sin"), sem("par_done")
        x_in = sems("x_in", XBUFS_A)
        x1_in = sems("x1_in", XBUFS_B)
        x1_stored = sems("x1_stored", XBUFS_A)
        out_stored = sems("out_stored", XBUFS_B)
        stage_in = sems("stage_in", STAGE)
        stage_b_in = sems("stage_b_in", STAGE_B)
        w_hi_done, w_lo_done = sem("w_hi_done"), sem("w_lo_done")
        v_dma = sems("v_dma", 2)
        stats_done, eps_done, rstd_done, xn_done = (sem(n) for n in ("stats_done", "eps_done", "rstd_done", "xn_done"))
        stats_raw = sem("stats_raw")
        x_biased = sem("x_biased")
        xt_psum, xt_hi_done, xt_lo_done = sem("xt_psum"), sem("xt_hi_done"), sem("xt_lo_done")
        q_psum, q_hi_done, q_lo_done = sem("q_psum"), sem("q_hi_done"), sem("q_lo_done")
        k_masked_done, kbd_hi_done, kbd_lo_done = sem("k_masked_done"), sem("kbd_hi_done"), sem("kbd_lo_done")
        v_masked_done, vbd_hi_done, vbd_lo_done = sem("v_masked_done"), sem("vbd_hi_done"), sem("vbd_lo_done")
        s_psum, clip_done, square_done = sem("s_psum"), sem("clip_done"), sem("square_done")
        top_done, shift_done, exp_done = sem("top_done"), sem("shift_done"), sem("exp_done")
        total_done, inv_done, prob_done = sem("total_done"), sem("inv_done"), sem("prob_done")
        pt_psum, pt_hi_done, pt_lo_done = sem("pt_psum"), sem("pt_hi_done"), sem("pt_lo_done")
        o_psum, o_hi_done, o_lo_done = sem("o_psum"), sem("o_hi_done"), sem("o_lo_done")
        y_psum, y_done = sem("y_psum"), sem("y_done")
        nan_step, nan_psum, nan_count, guard_done = (sem(n) for n in ("nan_step", "nan_psum", "nan_count", "guard_done"))
        fix_in, fix_add, fix_out = sem("fix_in"), sem("fix_add"), sem("fix_out")
        h_psum, turns_done, hid_done = sem("h_psum"), sem("turns_done"), sem("hid_done")
        whole_done, frac_done, sin_done = sem("whole_done"), sem("frac_done"), sem("sin_done")
        wave_done, act_hi_done, act_lo_done = sem("wave_done"), sem("act_hi_done"), sem("act_lo_done")
        f_psum, y2_done = sem("f_psum"), sem("y2_done")

        freed_by = {"xt": xt_lo_done, "q": q_lo_done, "pt": pt_lo_done, "o": o_lo_done, "y": y_done, "h": hid_done}

        chunks = [(wq[k * P:(k + 1) * P, :], wq_hi[:, k, :], wq_lo[:, k, :], SCALE) for k in range(KC)]
        chunks += [(wo[k * P:(k + 1) * P, :], wo_hi[:, k, :], wo_lo[:, k, :], 1.0) for k in range(KC)]
        chunks += [(w1[f], w1a_hi[:, f], w1a_lo[:, f], 1.0) for f in range(HALF1)]
        CHUNKS_A = len(chunks)
        w2_chunk, w1_chunk = {}, {f: 2 * KC + f for f in range(HALF1)}
        for f in range(FC):
            w2_chunk[f] = len(chunks)
            chunks.append((w2[f * P:(f + 1) * P, :], w2_hi[:, f, :], w2_lo[:, f, :], 1.0))
            if f < FC - HALF1:
                w1_chunk[HALF1 + f] = len(chunks)
                chunks.append((w1[HALF1 + f], w1b_hi[:, f], w1b_lo[:, f], 1.0))

        def staged(c):
            if c < CHUNKS_A:
                return stage[:, c % STAGE, :], stage_in[c % STAGE], 16 * (c // STAGE + 1)
            n = c - CHUNKS_A
            return stage_b[:, n % STAGE_B, :], stage_b_in[n % STAGE_B], 16 * (n // STAGE_B + 1)

        def like(flat, ap):
            return flat.rearrange("p (k m) -> p k m", m=P) if len(ap.shape) == 3 else flat

        def split_hi(act, need, c):
            raw, loaded, value = staged(c)
            _, hi, _, scale = chunks[c]
            need(loaded, value)
            act.activation(hi, like(raw, hi), ACT.Copy, scale=scale).then_inc(w_hi_done, 1)

        def split_lo(dve, need, c):
            raw, loaded, value = staged(c)
            _, hi, lo, scale = chunks[c]
            need(loaded, value)
            need(w_hi_done, c + 1)
            dve.scalar_tensor_tensor(out=lo, in0=like(raw, lo), scalar=scale, in1=hi.bitcast(F32), op0=ALU.mult,
                                     op1=ALU.subtract).then_inc(w_lo_done, 1)

        def x_tile(T):
            if T < TILES:
                return x_sb_a[T % XBUFS_A], x_in[T % XBUFS_A], 16 * (T // XBUFS_A + 1)
            t = T - TILES
            return x_sb[t % XBUFS_B], x1_in[t % XBUFS_B], 16 * (t // XBUFS_B + 1)

        def load_values(queue, need, b):
            if b >= 2:
                need(v_masked_done, KC * (b - 1))
            for half in range(2):
                queue.dma_start(v_in[half * KEYS:(half + 1) * KEYS, b % 2, :], v_dram[b]).then_inc(v_dma[b % 2], 16)

        def later_chunks(j):
            first = CHUNKS_A + 2 + 2 * j
            return range(min(first, len(chunks)), min(first + 2, len(chunks)))

        def residual(dve, need, t):
            tile = x_sb[t % XBUFS_B]
            need(x_biased, TILES + t + 1)
            need(f_psum, FC * (t + 1))
            for n in range(NB):
                dve.tensor_tensor(tile[:, n, :], psum[:, Y_BANK + n, :], tile[:, n, :], ALU.add).then_inc(y2_done, 1)

        block = stack.enter_context(nc.Block())

        @block.sync
        def _(sp):
            need = Waits(sp)

            def load_x(t):
                if t >= XBUFS_A:
                    need(x1_stored[t % XBUFS_A], 16 * (t // XBUFS_A))
                sp.dma_start(x_sb_a[t % XBUFS_A][:], x_rows[t]).then_inc(x_in[t % XBUFS_A], 16)

            def load_chunk(c):
                raw, loaded, _ = staged(c)
                if c < CHUNKS_A:
                    if c >= STAGE:
                        need(w_lo_done, c - STAGE + 1)
                elif c - CHUNKS_A >= STAGE_B:
                    need(w_lo_done, c - STAGE_B + 1)
                sp.dma_start(like(raw, chunks[c][1]), chunks[c][0]).then_inc(loaded, 16)

            sp.dma_start(ctx_sb[:], ctx_768.rearrange("(n b) k c -> (b k) n c", b=2)).then_inc(ctx_in, 16)
            load_x(0)
            load_chunk(0)
            load_chunk(1)
            sp.dma_start(wk_sb[:], wk.rearrange("(k p) c -> p k c", p=P)).then_inc(kw_in, 16)
            load_chunk(2)
            load_chunk(3)
            sp.dma_start(wv_sb[:], wv.rearrange("(k p) c -> p k c", p=P)).then_inc(vw_in, 16)
            load_x(1)
            for c in range(STAGE, 2 * KC):
                load_chunk(c)
            load_x(2)
            need(vn_psum, B // 2)
            need(vn_stored, 16 * (B // 2))
            need(vm_psum, 1)
            for b in range(2):
                load_values(sp, need, b)
            for t in range(TILES):
                if t < HALF1:
                    load_chunk(2 * KC + t)
                if t % TPB == 0 and TPB <= t < TILES - TPB:
                    load_values(sp, need, t // TPB + 1)
                need(y_done, NB * (t + 1))
                sp.dma_start(x1_rows[t], x_sb_a[t % XBUFS_A][:]).then_inc(x1_stored[t % XBUFS_A], 16)
                if t + XBUFS_A < TILES:
                    load_x(t + XBUFS_A)

            need(y_done, NB * TILES)
            need(guard_done, 1)
            for t in range(XBUFS_B):
                sp.dma_start(x_sb[t][:], x1_rows[t]).then_inc(x1_in[t], 16)
            sp.dma_start(b2_row[:], b2.partition_broadcast(P)).then_inc(b2_in, 16)
            for c in range(CHUNKS_A, len(chunks)):
                load_chunk(c)
            for t in range(TILES):
                slot = t % XBUFS_B
                need(y2_done, NB * (t + 1))
                sp.dma_start(out_rows[t], x_sb[slot][:]).then_inc(out_stored[slot], 16)
                if t + XBUFS_B < TILES:
                    need(out_stored[slot], 16 * (t // XBUFS_B + 1))
                    sp.dma_start(x_sb[slot][:], x1_rows[t + XBUFS_B]).then_inc(x1_in[slot], 16)
            for slot in range(XBUFS_B):
                need(out_stored[slot], 16 * (TILES // XBUFS_B))
            need(u_stored, 16 * KC)

        @block.gpsimd
        def _(pool):
            need = Waits(pool)
            made = 0

            def const(instruction):
                nonlocal made
                made += 1
                instruction.then_inc(const_ready, 1)
                need(const_ready, made)

            def bias_row(dst, src):
                pool.dma_start(dst[:], src.partition_broadcast(P)).then_inc(bias_in, 16)

            def by_channel(dst, src, s):
                pool.dma_start(dst, src).then_inc(s, 16)

            const(pool.memset(ident[:], 0.0))
            const(pool.memset(minus_half[:], -0.5))
            const(pool.memset(mask_k[:], 1.0))
            const(pool.memset(mask_v[:], 1.0))
            const(pool.memset(ones[:], 1.0))
            const(pool.memset(pick[:], 1.0 / KEYS))
            const(pool.affine_select(out=ident[:], in_=ident[:], compare_op=ALU.not_equal, fill=1.0, base=0,
                                     pattern=[[-1, P]], channel_multiplier=1))
            const(pool.affine_select(out=mask_k[:], in_=mask_k[:], compare_op=ALU.is_ge, fill=0.0, base=0,
                                     pattern=[[-D, HG]], channel_multiplier=1))
            for half in range(2):
                rows = slice(half * KEYS, (half + 1) * KEYS)
                const(pool.affine_select(out=mask_v[rows], in_=mask_v[rows], compare_op=ALU.is_ge, fill=0.0,
                                         base=-D * half, pattern=[[-2 * D, PAIRS], [1, P]], channel_multiplier=0))
                const(pool.memset(pick[rows, 1 - half:2 - half], 0.0))
            const(pool.affine_select(out=mask_k[:], in_=mask_k[:], compare_op=ALU.is_ge, fill=0.0, base=D - 1,
                                     pattern=[[D, HG]], channel_multiplier=-1))
            for half in range(2):
                rows = slice(half * KEYS, (half + 1) * KEYS)
                const(pool.affine_select(out=mask_v[rows], in_=mask_v[rows], compare_op=ALU.is_ge, fill=0.0,
                                         base=D * half + D - 1, pattern=[[2 * D, PAIRS], [-1, P]],
                                         channel_multiplier=0))
            assert made == CONSTS
            by_channel(bq_sb[:], bq, bias_in)
            by_channel(bk_sb[:], bk, bias_in)
            by_channel(bo_col[:], bo, bias_in)
            bias_row(bv_row, bv)
            bias_row(bo_row, bo_row_in)
            for n, vector in enumerate((phases, w_real, w_imag, b1)):
                by_channel(par[:, n, :], vector, par_in)

            def rsqrt(T):
                s = T % 2
                need(stats_done, T + 1)
                if T >= 2:
                    need(xn_done, T - 1)
                need(const_ready, CONSTS)
                pool.tensor_scalar(var_eps[:, s, :], mv[:, s, :, 1], EPS, 1.0, ALU.add, ALU.mult)\
                    .then_inc(eps_done, 1)
                need(eps_done, T + 1)
                pool.tensor_tensor(rstd[:, s, :], var_eps[:, s, :], minus_half[:], ALU.pow).then_inc(rstd_done, 1)

            def add_bias(t):
                tile, loaded, value = x_tile(t)
                need(xn_done, t + 1)
                need(bias_in, 80)
                pool.tensor_tensor(tile[:], tile[:], bo_row[:].unsqueeze(1).to_broadcast([P, NB, C]),
                                   ALU.add).then_inc(x_biased, 1)

            def add_bias_b(t):
                tile, loaded, value = x_tile(TILES + t)
                need(xn_done, TILES + t + 1)
                need(b2_in, 16)
                pool.tensor_tensor(tile[:], tile[:], b2_row[:].unsqueeze(1).to_broadcast([P, NB, C]),
                                   ALU.add).then_inc(x_biased, 1)

            def mask_keys(b, g):
                n = b * KC + g
                need(kt_done, KC)
                if n:
                    need(kbd_lo_done, n)
                pool.tensor_tensor(k_masked[:], kt[:, g, b * KEYS:(b + 1) * KEYS].unsqueeze(1).to_broadcast([P, HG, KEYS]),
                                   mask_k[:].unsqueeze(2).to_broadcast([P, HG, KEYS]), ALU.mult)\
                    .then_inc(k_masked_done, 1)

            def mask_values(b, g):
                n = b * KC + g
                need(v_dma[b % 2], 32 * (b // 2 + 1))
                if n:
                    need(vbd_lo_done, n)
                pool.tensor_tensor(v_masked[:], v_in[:, b % 2, g * P:(g + 1) * P].unsqueeze(1).to_broadcast([P, PAIRS, P]),
                                   mask_v[:], ALU.mult).then_inc(v_masked_done, 1)

            rsqrt(0)
            for g in range(KC):
                mask_keys(0, g)
            for n in range(B // 2):
                need(vn_done, n + 1)
                pool.dma_start(v_dram[2 * n:2 * n + 2].rearrange("b k c -> (b k) c"), v_sb[:, 0, :])\
                    .then_inc(vn_stored, 16)
            for g in range(KC):
                mask_values(0, g)

            def shift(i):
                need(top_done, i + 1)
                rows = prob[:, i % SCORE_BUFS]
                pool.tensor_tensor(rows, rows, top[:, i % 2, :].unsqueeze(2).to_broadcast([P, NB * HG, KEYS]),
                                   ALU.subtract).then_inc(shift_done, 1)

            def normalise(i):
                need(inv_done, i + 1)
                rows = prob[:, i % SCORE_BUFS]
                pool.tensor_tensor(rows, rows, inv[:, i % 2, :].unsqueeze(2).to_broadcast([P, NB * HG, KEYS]),
                                   ALU.mult).then_inc(prob_done, 1)

            for i in range(GROUPS + LAG_A):
                t, g = divmod(i, KC)
                if 1 <= i <= GROUPS:
                    normalise(i - 1)
                if i < GROUPS:
                    shift(i)
                    if g == 0 and t + 1 < TILES:
                        rsqrt(t + 1)
                    if g == 3:
                        add_bias(t)
                    b = t // TPB + 1
                    if t % TPB == TPB - 1 and b < B:
                        mask_keys(b, g)
                late = i - LAG_A - 1
                if late >= 0:
                    t, g = divmod(late, KC)
                    b = t // TPB + 1
                    if t % TPB == TPB - 1 and b < B:
                        mask_values(b, g)
                if i == KC:
                    need(u_done, 1)
                    for k in range(KC):
                        pool.dma_start(u_dram[:, k * P:(k + 1) * P].rearrange("b p -> p b"), u_sb[:, k, :],
                                       allow_slow_non_contiguous=True).then_inc(u_stored, 16)

            for slot in range(XBUFS_A):
                need(x1_stored[slot], 16 * len(range(slot, TILES, XBUFS_A)))
            need(u_stored, 16 * KC)
            need(nan_count, 1)
            count = pool.alloc_register("rows_without_nan")
            pool.reg_load(count, ok_count[0:1, 0:1])
            with pool.If_ne(count, P):
                for t in range(TILES):
                    if t:
                        pool.wait_ge(fix_out, 16 * t)
                    pool.dma_start(x_sb[0][:], x_rows[t]).then_inc(fix_in, 16)
                    pool.dma_start(x_sb[1][:, 0, :], u_dram[t // TPB].partition_broadcast(P)).then_inc(fix_in, 16)
                    pool.wait_ge(fix_in, 32 * (t + 1))
                    pool.tensor_tensor(x_sb[0][:], x_sb[0][:], x_sb[1][:, 0:1, :].to_broadcast([P, NB, C]), ALU.add)\
                        .then_inc(fix_add, 1)
                    pool.wait_ge(fix_add, t + 1)
                    pool.dma_start(x1_rows[t], x_sb[0][:]).then_inc(fix_out, 16)
                pool.wait_ge(fix_out, 16 * TILES)
            pool.memset(ones[:], 1.0).then_inc(guard_done, 1)

            rsqrt(TILES)
            add_bias_b(0)
            for t in range(TILES):
                for f in range(FC):
                    j = t * FC + f
                    need(whole_done, j + 1)
                    pool.tensor_tensor(frac[:, j % 2, :], turns[:, j % 2, :], frac[:, j % 2, :], ALU.subtract)\
                        .then_inc(frac_done, 1)
                    if f == LN_AT and t + 1 < TILES:
                        rsqrt(TILES + t + 1)
                    if f == LN_AT + 4 and t + 1 < TILES:
                        add_bias_b(t + 1)

        @block.scalar
        def _(act):
            need = Waits(act)

            def param_sines():
                need(par_step, PAR_REDUCED)
                act.activation(red[:, 5, :], red[:, 3, :], ACT.Sin)
                act.activation(red[:, 6, :], red[:, 4, :], ACT.Sin).then_inc(par_sin, 1)

            def xt_to_hi(n):
                T, k = divmod(n, KC)
                need(xt_psum, n + 1)
                if 0 < T < TILES:
                    need(q_psum, KC * T)
                elif T == TILES:
                    need(q_psum, GROUPS)
                elif T > TILES:
                    need(h_psum, FC * (T - TILES))
                act.activation(xt_hi[:, k, :], bank(("xt", n)), ACT.Copy).then_inc(xt_hi_done, 1)

            for g in range(KC):
                need(kt_psum, g + 1)
                need(bias_in, 80)
                act.activation(kt[:, g, :], psum[:, g, :], ACT.Identity, bias=bk_sb[:, g:g + 1]).then_inc(kt_done, 1)
                split_hi(act, need, g)
            for k in range(KC):
                xt_to_hi(k)

            def q_to_hi(i):
                need(q_psum, i + 1)
                need(bq_scaled, 1)
                if i >= 2:
                    need(s_psum, S_BANKS * (i - 1))
                act.activation(q_hi[:, i % 2, :], bank(("q", i)), ACT.Identity, bias=bq_sb[:, i % KC:i % KC + 1])\
                    .then_inc(q_hi_done, 1)

            def keys_to_hi(b, g):
                need(k_masked_done, b * KC + g + 1)
                if b:
                    need(s_psum, S_BANKS * ((b - 1) * GB + GB - KC + g + 1))
                act.activation(kbd_hi[:, g, :], k_masked[:].rearrange("p h k -> p (h k)"), ACT.Copy)\
                    .then_inc(kbd_hi_done, 1)

            def values_to_hi(b, g):
                need(v_masked_done, b * KC + g + 1)
                if b:
                    need(o_psum, (b - 1) * GB + GB - KC + g + 1)
                act.activation(vbd_hi[:, g], v_masked[:], ACT.Copy).then_inc(vbd_hi_done, 1)

            for g in range(KC):
                keys_to_hi(0, g)
            q_to_hi(0)
            for c in range(KC, 2 * KC):
                split_hi(act, need, c)
            need(vm_done, 1)
            act.activation(vm_hi[:], v_mean[:], ACT.Copy).then_inc(vm_hi_done, 1)
            for g in range(KC):
                values_to_hi(0, g)

            for i in range(GROUPS + LAG_A):
                t, g = divmod(i, KC)
                late = i - LAG_A
                if 1 <= i <= GROUPS:
                    need(shift_done, i)
                    rows = prob[:, (i - 1) % SCORE_BUFS]
                    act.activation(rows, rows, ACT.Exp).then_inc(exp_done, 1)
                if late >= 0:
                    for n in range(late * PAIRS, (late + 1) * PAIRS):
                        need(pt_psum, n + 1)
                        need(o_psum, late)
                        act.activation(pt_hi[:, n % PAIRS, :], bank(("pt", n)), ACT.Copy).then_inc(pt_hi_done, 1)
                if i < GROUPS:
                    for n in range(S_BANKS * i, S_BANKS * (i + 1)):
                        need(clip_done, n + 1)
                        if n >= 2:
                            need(square_done, n - 1)
                        act.activation(square[:, n % 2, :], psum[:, n % S_BANKS, :], ACT.Square,
                                       accum_out=squares[:, n:n + 1]).then_inc(square_done, 1)
                if i + 1 < GROUPS:
                    q_to_hi(i + 1)
                if i % KC == KC - 2 and i + 2 < GROUPS:
                    for k in range(KC):
                        xt_to_hi((t + 1) * KC + k)
                if late >= 0:
                    need(o_psum, late + 1)
                    if late >= KC:
                        need(y_psum, NB * (late // KC))
                    act.activation(o_hi[:, late % KC, :], bank(("o", late)), ACT.Copy).then_inc(o_hi_done, 1)
                if i < GROUPS:
                    b = t // TPB + 1
                    if t % TPB == TPB - 1 and b < B:
                        keys_to_hi(b, g)
                if late - 1 >= 0:
                    tt, gg = divmod(late - 1, KC)
                    b = tt // TPB + 1
                    if tt % TPB == TPB - 1 and b < B:
                        values_to_hi(b, gg)
                if i % KC == 1 and t < HALF1:
                    split_hi(act, need, 2 * KC + t)

            param_sines()
            for k in range(KC):
                xt_to_hi(TILES * KC + k)

            def finish(j):
                need(frac_done, j + 1)
                act.activation(frac[:, j % 2, :], frac[:, j % 2, :], ACT.Sin, scale=SIN_SCALE).then_inc(sin_done, 1)
                need(wave_done, j + 1)
                if j >= ACTS:
                    need(f_psum, j - ACTS + 1)
                act.activation(act_hi[:, j % ACTS, :], hid[:, j % 2, :], ACT.Relu).then_inc(act_hi_done, 1)

            for c in range(CHUNKS_A, CHUNKS_A + 2):
                split_hi(act, need, c)
            for j in range(TILES * FC):
                t, f = divmod(j, FC)
                need(h_psum, j + 1)
                if j >= 2:
                    need(frac_done, j - 1)
                    need(act_lo_done, j - 1)
                act.activation(turns[:, j % 2, :], bank(("h", j)), ACT.Identity, bias=u_shift[:, f:f + 1],
                               scale=0.1 / TWO_PI).then_inc(turns_done, 1)
                act.activation(hid[:, j % 2, :], bank(("h", j)), ACT.Identity, bias=par[:, 3, f:f + 1])\
                    .then_inc(hid_done, 1)
                if j:
                    finish(j - 1)
                if j < FC:
                    for c in later_chunks(j):
                        split_hi(act, need, c)
                if f == FC - 1 and t + 1 < TILES:
                    for k in range(KC):
                        xt_to_hi((TILES + t + 1) * KC + k)
            finish(TILES * FC - 1)

        @block.vector
        def _(dve):
            need = Waits(dve)
            steps = 0

            def par_scalar(dst, src, *scalars_and_ops):
                nonlocal steps
                steps += 1
                dve.tensor_scalar(dst, src, *scalars_and_ops).then_inc(par_step, 1)
                need(par_step, steps)

            def par_tensor(dst, in0, scalar, in1, op0, op1):
                nonlocal steps
                steps += 1
                dve.scalar_tensor_tensor(out=dst, in0=in0, scalar=scalar, in1=in1, op0=op0, op1=op1)\
                    .then_inc(par_step, 1)
                need(par_step, steps)

            def layer_stats(T):
                tile, loaded, value = x_tile(T)
                need(loaded, value)
                if T >= 2:
                    need(rstd_done, T - 1)
                for n in range(NB):
                    last = dve.bn_stats(stats[:, T % 2, n, :], tile[:, n, :])
                last.then_inc(stats_raw, 1)
                need(stats_raw, T + 1)
                for n in range(NB):
                    last = dve.bn_aggr(mv[:, T % 2, n, :], stats[:, T % 2, n, :])
                last.then_inc(stats_done, 1)

            def layer_rows(T):
                tile, loaded, value = x_tile(T)
                need(rstd_done, T + 1)
                need(stats_done, T + 1)
                if T:
                    need(xt_psum, KC * T)
                for n in range(NB):
                    last = dve.tensor_scalar(xn[:, n, :], tile[:, n, :], mv[:, T % 2, n, 0:1], rstd[:, T % 2, n:n + 1],
                                             ALU.subtract, ALU.mult)
                last.then_inc(xn_done, 1)

            def xt_to_lo(n):
                T, k = divmod(n, KC)
                need(xt_hi_done, n + 1)
                dve.tensor_tensor(xt_lo[:, k, :], bank(("xt", n)), xt_hi[:, k, :].bitcast(F32), ALU.subtract)\
                    .then_inc(xt_lo_done, 1)

            theta, w_re, w_im, bias1 = (par[:, n, :] for n in range(4))

            def phases_reduced():
                need(par_in, 64)

                def reduce_phase(dst, src, tmp):
                    par_scalar(tmp, src, 1.0 / TWO_PI, ROUND, ALU.mult, ALU.add)
                    par_scalar(tmp, tmp, ROUND, None, ALU.subtract)
                    par_tensor(dst, tmp, -PI_A, src, ALU.mult, ALU.add)
                    par_tensor(dst, tmp, -PI_B, dst, ALU.mult, ALU.add)
                    par_tensor(dst, tmp, -PI_C, dst, ALU.mult, ALU.add)

                reduce_phase(red[:, 1, :], theta, red[:, 0, :])
                par_scalar(red[:, 2, :], red[:, 1, :], math.pi / 2, None, ALU.add)
                reduce_phase(red[:, 7, :], red[:, 2, :], red[:, 0, :])
                pi_down = 3.1415925
                par_scalar(red[:, 3, :], red[:, 1, :], pi_down, -pi_down, ALU.min, ALU.max)
                par_scalar(red[:, 4, :], red[:, 7, :], pi_down, -pi_down, ALU.min, ALU.max)
                assert steps == PAR_REDUCED
                par_tensor(red[:, 2, :], bias1, 0.1, red[:, 1, :], ALU.mult, ALU.add)
                par_scalar(u_shift[:], red[:, 2, :], 1.0 / TWO_PI, None, ALU.mult)

            def phases_gain():
                need(par_sin, 1)
                par_tensor(red[:, 0, :], red[:, 6, :], 1.0, w_re, ALU.mult, ALU.mult)
                par_tensor(red[:, 2, :], red[:, 5, :], 1.0, w_im, ALU.mult, ALU.mult)
                par_tensor(red[:, 0, :], red[:, 0, :], 1.0, red[:, 2, :], ALU.mult, ALU.add)
                par_tensor(gain[:], red[:, 0, :], 0.1, w_im, ALU.mult, ALU.mult)

            for k in range(KK):
                need(ctxt_psum, k + 1)
                dve.tensor_copy(ctxt[:, k, :], psum[:, k, :]).then_inc(ctxt_done, 1)
            layer_stats(0)
            need(bias_in, 80)
            dve.tensor_scalar(bq_sb[:], bq_sb[:], SCALE, None, ALU.mult).then_inc(bq_scaled, 1)
            layer_rows(0)
            for c in range(KC):
                split_lo(dve, need, c)
            for k in range(KC):
                xt_to_lo(k)

            def q_to_lo(i):
                need(q_hi_done, i + 1)
                need(bq_scaled, 1)
                dve.scalar_tensor_tensor(out=q_lo[:, i % 2, :], in0=bank(("q", i)), scalar=bq_sb[:, i % KC:i % KC + 1],
                                         in1=q_hi[:, i % 2, :].bitcast(F32), op0=ALU.add, op1=ALU.subtract)\
                    .then_inc(q_lo_done, 1)

            def keys_to_lo(b, g):
                need(kbd_hi_done, b * KC + g + 1)
                dve.tensor_tensor(kbd_lo[:, g, :], k_masked[:].rearrange("p h k -> p (h k)"),
                                  kbd_hi[:, g, :].bitcast(F32), ALU.subtract).then_inc(kbd_lo_done, 1)

            def values_to_lo(b, g):
                need(vbd_hi_done, b * KC + g + 1)
                dve.tensor_tensor(vbd_lo[:, g], v_masked[:], vbd_hi[:, g].bitcast(F32), ALU.subtract)\
                    .then_inc(vbd_lo_done, 1)

            for g in range(KC):
                keys_to_lo(0, g)
            q_to_lo(0)
            for n in range(B // 2):
                need(vn_psum, n + 1)
                if n:
                    need(vn_stored, 16 * n)
                    need(vm_pair, n)
                dve.tensor_tensor(v_sb[:, 0, :], psum[:, VN_BANK, :], bv_row[:], ALU.add).then_inc(vn_done, 1)
            for c in range(KC, 2 * KC):
                split_lo(dve, need, c)
            need(vm_psum, 1)
            dve.tensor_copy(v_mean[:], psum[:, VM_BANK, 0:KC * B].rearrange("p (k b) -> p k b", b=B)).then_inc(vm_done, 1)
            need(vm_hi_done, 1)
            need(vm_done, 1)
            dve.tensor_tensor(vm_lo[:], v_mean[:], vm_hi[:].bitcast(F32), ALU.subtract).then_inc(vm_lo_done, 1)
            need(u_psum, 1)
            dve.tensor_tensor(u_sb[:], psum[:, U_BANK, 0:KC * B].rearrange("p (k b) -> p k b", b=B),
                              bo_col[:].unsqueeze(2).to_broadcast([P, KC, B]), ALU.add).then_inc(u_done, 1)
            for g in range(KC):
                values_to_lo(0, g)

            for i in range(GROUPS + LAG_A):
                t, g = divmod(i, KC)
                late = i - LAG_A
                if i < GROUPS:
                    if i >= SCORE_BUFS:
                        need(pt_psum, PAIRS * (i - SCORE_BUFS + 1))
                    for n in range(S_BANKS * i, S_BANKS * (i + 1)):
                        need(s_psum, n + 1)
                        half = n % S_BANKS
                        rows = NB * HG // S_BANKS
                        dve.tensor_scalar(prob[:, i % SCORE_BUFS, half * rows:(half + 1) * rows, :]
                                          .rearrange("p h k -> p (h k)"), psum[:, half, :], CLAMP, -CLAMP,
                                          ALU.min, ALU.max).then_inc(clip_done, 1)
                if late >= 0:
                    for n in range(late * PAIRS, (late + 1) * PAIRS):
                        need(pt_hi_done, n + 1)
                        dve.tensor_tensor(pt_lo[:, n % PAIRS, :], bank(("pt", n)), pt_hi[:, n % PAIRS, :].bitcast(F32),
                                          ALU.subtract).then_inc(pt_lo_done, 1)
                if 1 <= i <= GROUPS:
                    e = i - 1
                    need(exp_done, e + 1)
                    if e >= 2:
                        need(prob_done, e - 1)
                    dve.reduce_sum(total[:, e % 2, :], prob[:, e % SCORE_BUFS], AX_X).then_inc(total_done, 1)
                if i < GROUPS:
                    need(clip_done, S_BANKS * (i + 1))
                    if i >= 2:
                        need(shift_done, i - 1)
                    dve.reduce_max(top[:, i % 2, :], prob[:, i % SCORE_BUFS], AX_X).then_inc(top_done, 1)
                if 1 <= i <= GROUPS:
                    need(total_done, i)
                    dve.reciprocal(inv[:, (i - 1) % 2, :], total[:, (i - 1) % 2, :]).then_inc(inv_done, 1)
                if i + 1 < GROUPS:
                    q_to_lo(i + 1)
                if i % KC == KC - 2 and i + 2 < GROUPS:
                    for k in range(KC):
                        xt_to_lo((t + 1) * KC + k)
                if late >= 0:
                    need(o_hi_done, late + 1)
                    dve.tensor_tensor(o_lo[:, late % KC, :], bank(("o", late)), o_hi[:, late % KC, :].bitcast(F32),
                                      ALU.subtract).then_inc(o_lo_done, 1)
                if g == 0 and t + 1 < TILES:
                    layer_stats(t + 1)
                if g == 1 and t + 1 < TILES:
                    layer_rows(t + 1)
                if late >= 0 and late % KC == KC - 1:
                    tt = late // KC
                    need(x_biased, tt + 1)
                    for n in range(NB):
                        need(y_psum, tt * NB + n + 1)
                        tile = x_sb_a[tt % XBUFS_A]
                        dve.tensor_tensor(tile[:, n, :], bank(("y", tt * NB + n)), tile[:, n, :], ALU.add)\
                            .then_inc(y_done, 1)
                if i < GROUPS:
                    b = t // TPB + 1
                    if t % TPB == TPB - 1 and b < B:
                        keys_to_lo(b, g)
                if late - 1 >= 0:
                    tt, gg = divmod(late - 1, KC)
                    b = tt // TPB + 1
                    if tt % TPB == TPB - 1 and b < B:
                        values_to_lo(b, gg)
                if i % KC == 1 and t < HALF1:
                    split_lo(dve, need, 2 * KC + t)
                if i == KC:
                    phases_reduced()
                if i == GROUPS:
                    need(square_done, S_BANKS * GROUPS)
                    dve.tensor_tensor(not_nan[:], squares[:], squares[:], ALU.is_equal).then_inc(nan_step, 1)
                    need(nan_step, 1)
                    dve.tensor_reduce(row_ok[:], not_nan[:], AX_X, ALU.min).then_inc(nan_step, 1)
            need(nan_psum, 1)
            dve.tensor_copy(ok_count[:], psum[0:1, 0, 0:1]).then_inc(nan_count, 1)

            phases_gain()
            layer_stats(TILES)
            layer_rows(TILES)
            for k in range(KC):
                xt_to_lo(TILES * KC + k)

            def finish(j):
                need(sin_done, j + 1)
                need(hid_done, j + 1)
                f = j % FC
                dve.scalar_tensor_tensor(out=hid[:, j % 2, :], in0=frac[:, j % 2, :], scalar=gain[:, f:f + 1],
                                         in1=hid[:, j % 2, :], op0=ALU.mult, op1=ALU.add).then_inc(wave_done, 1)
                need(act_hi_done, j + 1)
                dve.scalar_tensor_tensor(out=act_lo[:, j % ACTS, :], in0=hid[:, j % 2, :], scalar=0.0,
                                         in1=act_hi[:, j % ACTS, :].bitcast(F32), op0=ALU.max, op1=ALU.subtract)\
                    .then_inc(act_lo_done, 1)

            for c in range(CHUNKS_A, CHUNKS_A + 2):
                split_lo(dve, need, c)
            for j in range(TILES * FC):
                t, f = divmod(j, FC)
                need(turns_done, j + 1)
                if j >= 2:
                    need(wave_done, j - 1)
                dve.tensor_scalar(frac[:, j % 2, :], turns[:, j % 2, :], ROUND, ROUND, ALU.add, ALU.subtract)\
                    .then_inc(whole_done, 1)
                if j:
                    finish(j - 1)
                if j < FC:
                    for c in later_chunks(j):
                        split_lo(dve, need, c)
                if f == LN_AT and t + 1 < TILES:
                    layer_stats(TILES + t + 1)
                if f == LN_AT + 2 and t + 1 < TILES:
                    layer_rows(TILES + t + 1)
                if f == FC - 1 and t + 1 < TILES:
                    for k in range(KC):
                        xt_to_lo((TILES + t + 1) * KC + k)
                if f == LAG_B - 1 and t > 0:
                    residual(dve, need, t - 1)
            finish(TILES * FC - 1)
            residual(dve, need, TILES - 1)

        @block.tensor
        def _(pe):
            need = Waits(pe)

            def product(o, stationary, moving, first=True, last=True):
                (a_hi, a_lo), (b_hi, b_lo) = stationary, moving
                for n, (a, b_) in enumerate(((a_hi, b_hi), (a_hi, b_lo), (a_lo, b_hi))):
                    m = pe.matmul(o, a, b_, start=first and n == 0, stop=last and n == 2)
                return m

            def bank_free(item):
                prior = before[item]
                if prior:
                    need(freed_by[prior[0]], prior[1] + 1)

            need(const_ready, CONSTS)
            need(ctx_in, 16)
            for k in range(KK):
                for n in range(B // 2):
                    m = pe.transpose(psum[:, k, n * P:(n + 1) * P], ctx_sb[:, n, k * P:(k + 1) * P], ident[:])
                m.then_inc(ctxt_psum, 1)
            need(kw_in, 16)
            need(ctxt_done, KK)
            for g in range(KC):
                for k in range(KK):
                    m = pe.matmul(psum[:, g, :], wk_sb[:, k, g * P:(g + 1) * P], ctxt[:, k, :], start=k == 0, stop=k == KK - 1)
                m.then_inc(kt_psum, 1)

            def xt(n):
                T, k = divmod(n, KC)
                need(xn_done, T + 1)
                bank_free(("xt", n))
                for blk in range(NB):
                    m = pe.transpose(bank(("xt", n))[:, blk * P:(blk + 1) * P], xn[:, blk, k * P:(k + 1) * P], ident[:])
                m.then_inc(xt_psum, 1)

            def q(i):
                t, g = divmod(i, KC)
                need(w_lo_done, KC)
                bank_free(("q", i))
                for k in range(KC):
                    need(xt_lo_done, t * KC + k + 1)
                    cols = slice(g * P, (g + 1) * P)
                    m = product(bank(("q", i)), (wq_hi[:, k, cols], wq_lo[:, k, cols]), (xt_hi[:, k, :], xt_lo[:, k, :]),
                                k == 0, k == KC - 1)
                m.then_inc(q_psum, 1)

            def s(i):
                t, g = divmod(i, KC)
                need(q_lo_done, i + 1)
                need(kbd_lo_done, (t // TPB) * KC + g + 1)
                per_bank = BANK // SG
                for blk in range(NB):
                    half, at = divmod(blk, per_bank)
                    if i:
                        need(square_done, S_BANKS * (i - 1) + half + 1)
                    toks = slice(blk * P, (blk + 1) * P)
                    m = product(psum[:, half, at * SG:(at + 1) * SG], (q_hi[:, i % 2, toks], q_lo[:, i % 2, toks]),
                                (kbd_hi[:, g, :], kbd_lo[:, g, :]))
                    if at == per_bank - 1:
                        m.then_inc(s_psum, 1)

            def pt(n):
                i, j = divmod(n, PAIRS)
                need(prob_done, i + 1)
                bank_free(("pt", n))
                for blk in range(NB):
                    heads = slice(blk * HG + 2 * j, blk * HG + 2 * j + 2)
                    m = pe.transpose(bank(("pt", n))[:, blk * P:(blk + 1) * P],
                                     prob[:, i % SCORE_BUFS, heads, :].rearrange("p h k -> p (h k)"), ident[:])
                m.then_inc(pt_psum, 1)

            def o(i):
                t, g = divmod(i, KC)
                need(vbd_lo_done, (t // TPB) * KC + g + 1)
                bank_free(("o", i))
                for j in range(PAIRS):
                    need(pt_lo_done, PAIRS * i + j + 1)
                    m = product(bank(("o", i)), (vbd_hi[:, g, j, :], vbd_lo[:, g, j, :]), (pt_hi[:, j, :], pt_lo[:, j, :]),
                                j == 0, j == PAIRS - 1)
                m.then_inc(o_psum, 1)

            def y(n):
                t, blk = divmod(n, NB)
                need(w_lo_done, 2 * KC)
                bank_free(("y", n))
                toks = slice(blk * P, (blk + 1) * P)
                for g in range(KC):
                    need(o_lo_done, t * KC + g + 1)
                    m = product(bank(("y", n)), (o_hi[:, g, toks], o_lo[:, g, toks]), (wo_hi[:, g, :], wo_lo[:, g, :]),
                                g == 0, g == KC - 1)
                m.then_inc(y_psum, 1)

            def values():
                for n in range(B // 2):
                    need(vw_in, 16)
                    if n:
                        need(vn_done, n)
                    for k in range(KK):
                        m = pe.matmul(psum[:, VN_BANK, :], ctxt[:, k, n * P:(n + 1) * P], wv_sb[:, k, :], start=k == 0,
                                      stop=k == KK - 1)
                    m.then_inc(vn_psum, 1)
                    need(vn_done, n + 1)
                    for g in range(KC):
                        m = pe.matmul(psum[:, VM_BANK, g * B + 2 * n:g * B + 2 * n + 2], v_sb[:, 0, g * P:(g + 1) * P],
                                      pick[:], start=True, stop=True)
                    m.then_inc(vm_psum if n == B // 2 - 1 else vm_pair, 1)
                need(vm_lo_done, 1)
                need(w_lo_done, 2 * KC)
                for k in range(KC):
                    cols = slice(k * P, (k + 1) * P)
                    for g in range(KC):
                        m = product(psum[:, U_BANK, k * B:(k + 1) * B], (wo_hi[:, g, cols], wo_lo[:, g, cols]),
                                    (vm_hi[:, g, :], vm_lo[:, g, :]), g == 0, g == KC - 1)
                m.then_inc(u_psum, 1)

            run = {"xt": xt, "q": q, "s": s, "pt": pt, "o": o, "y": y}
            need(kt_done, KC)
            for kind, n in order_a:
                if (kind, n) == ("s", 0):
                    values()
                    need(u_done, 1)
                run[kind](n)
            need(nan_step, 2)
            need(square_done, S_BANKS * GROUPS)
            pe.matmul(psum[0:1, 0, 0:1], row_ok[:], ones[:], start=True, stop=True).then_inc(nan_psum, 1)

            def h(j):
                t, f = divmod(j, FC)
                need(w_lo_done, w1_chunk[f] + 1)
                bank_free(("h", j))
                hi, lo = (w1a_hi, w1a_lo) if f < HALF1 else (w1b_hi, w1b_lo)
                for k in range(KC):
                    need(xt_lo_done, (TILES + t) * KC + k + 1)
                    m = product(bank(("h", j)), (hi[:, f % HALF1, k, :], lo[:, f % HALF1, k, :]),
                                (xt_hi[:, k, :], xt_lo[:, k, :]), k == 0, k == KC - 1)
                m.then_inc(h_psum, 1)

            def f_(j):
                t, f = divmod(j, FC)
                need(w_lo_done, w2_chunk[f] + 1)
                need(act_lo_done, j + 1)
                if f == 0 and t:
                    need(y2_done, NB * t)
                for blk in range(NB):
                    toks = slice(blk * P, (blk + 1) * P)
                    m = product(psum[:, Y_BANK + blk, :], (act_hi[:, j % ACTS, toks], act_lo[:, j % ACTS, toks]),
                                (w2_hi[:, f, :], w2_lo[:, f, :]), f == 0, f == FC - 1)
                m.then_inc(f_psum, 1)

            need(nan_count, 1)
            need(y_done, NB * TILES)
            run = {"xt": xt, "h": h, "f": f_}
            for kind, n in order_b:
                run[kind](n)


def kernel(x, ctx_768, L0_xattn_Wq, L0_xattn_bq, L0_xattn_Wk, L0_xattn_bk, L0_xattn_Wv, L0_xattn_bv, L0_xattn_Wo,
           L0_xattn_bo, L0_ffn_W1, L0_ffn_b1, L0_ffn_quantum_phases, L0_ffn_quantum_weights_real,
           L0_ffn_quantum_weights_imag, L0_ffn_W2, L0_ffn_b2):
    import concourse.bacc as bacc
    from concourse.bass_utils import run_bass_kernel_spmd

    def by_channel(v):
        return np.asarray(v).reshape(-1, P).T

    w1_blocks = np.asarray(L0_ffn_W1).reshape(KC, P, FC, P).transpose(2, 1, 0, 3)
    laid_out = {
        "x": x, "ctx_768": ctx_768, "wq": L0_xattn_Wq, "bq": by_channel(L0_xattn_bq), "wk": L0_xattn_Wk,
        "bk": by_channel(L0_xattn_bk), "wv": L0_xattn_Wv, "bv": L0_xattn_bv, "wo": L0_xattn_Wo,
        "bo_row": L0_xattn_bo, "bo": by_channel(L0_xattn_bo), "w1": w1_blocks, "b1": by_channel(L0_ffn_b1),
        "phases": by_channel(L0_ffn_quantum_phases), "w_real": by_channel(L0_ffn_quantum_weights_real),
        "w_imag": by_channel(L0_ffn_quantum_weights_imag), "w2": L0_ffn_W2, "b2": L0_ffn_b2,
    }
    nc = bacc.Bacc("TRN2", target_bir_lowering=False, num_devices=1)
    arrays, args = {}, []
    for name, a in laid_out.items():
        a = np.ascontiguousarray(a)
        arrays[f"in_{name}"] = a
        args.append(nc.dram_tensor(f"in_{name}", a.shape, mybir.dt.from_np(a.dtype), kind="ExternalInput").ap())
    out = nc.dram_tensor("out", (B, N, C), F32, kind="ExternalOutput").ap()
    x1_dram = nc.dram_tensor("x1_dram", (B * N, C), F32, kind="Internal").ap()
    v_dram = nc.dram_tensor("v_dram", (B, KEYS, C), F32, kind="Internal").ap()
    u_dram = nc.dram_tensor("u_dram", (B, C), F32, kind="Internal").ap()
    xattn_ffn(nc, *args, out, x1_dram, v_dram, u_dram)
    r = run_bass_kernel_spmd(nc, [arrays], core_ids=[0])
    return r.results[0]["out"]
```

```python
from contextlib import ExitStack
import math

import numpy as np

import concourse.bass as bass
from concourse import mybir

F32 = mybir.dt.float32
F32R = mybir.dt.float32r
I32 = mybir.dt.int32
ALU = mybir.AluOpType
ACT = mybir.ActivationFunctionType
AX_X = mybir.AxisListType.X

P = 128
BANKS, BANK = 8, 512
B, N, C = 8, 1024, 512
HEADS, KEYS, CK = 16, 64, 384
FF = 2048
D = C // HEADS
SCALE = float(D) ** -0.5
CLAMP = 10000.0
EPS = 1e-5

TOK = 512
TILES = B * N // TOK
TPB = N // TOK
NB = TOK // P
KC = C // P
KK = CK // P
HG = P // D
GROUPS = TILES * KC
GB = TPB * KC
SG = HG * KEYS
PAIRS = HG // 2
FC = FF // P
HALF1 = FC // 2

ROUND = 1.5 * 2.0 ** 23
TWO_PI = 2.0 * math.pi
SIN_SCALE = 6.283185
PI_A = 6.28125
PI_B = float(np.float32(np.round((TWO_PI - PI_A) * 2.0 ** 20) / 2.0 ** 20))
PI_C = TWO_PI - PI_A - PI_B

LAG_A = 2
LAG_B = 3
SCORE_BUFS = 3
STAGE = 2
ACTS = LAG_B + 1
XBUFS = 2
O_BUFS = 7
M_STEP, U_STEP = 4, 6
STEPS_A = GROUPS + LAG_A + NB
LN_AT = 7
GUARDED = TILES - 2
CONSTS = 15
PAR_REDUCED = 13


class Waits:

    def __init__(self, engine):
        self.engine, self.seen = engine, {}

    def __call__(self, sem, value):
        if value > self.seen.get(id(sem), 0):
            self.engine.wait_ge(sem, value)
            self.seen[id(sem)] = value


def output_block(i):
    n = i - (LAG_A + KC)
    return n if 0 <= n < TILES * NB else None


def plan_phase_a():
    order = [("kt0", 0)] + [("xt", k) for k in range(KC)] + [("q", 0), ("v", 0)]
    spread = {0: [("k", 0), ("k", 1)], 1: [("k", 2), ("v", 1)], 2: [("k", 3), ("v", 2)], 3: [("v", 3)],
              M_STEP: [("m", 0)], U_STEP: [("u", 0)]}
    for i in range(STEPS_A):
        late = i - LAG_A
        if i < GROUPS:
            order.append(("s", i))
        if 0 <= late < GROUPS:
            order += [("pt", late * PAIRS + j) for j in range(PAIRS)]
        if i + 1 < GROUPS:
            order.append(("q", i + 1))
            if i % KC == KC - 2 and i + 2 < GROUPS:
                tile = i // KC + 1
                order += [("xt", tile * KC + k) for k in range(KC)]
        order += spread.get(i, [])
        if output_block(i) is not None:
            order.append(("y", output_block(i)))
        if 0 <= late < GROUPS:
            order.append(("o", late))
        if i == GROUPS:
            order.append(("nan", 0))
    return order


def plan_phase_b():
    order = [("xt", TILES * KC + k) for k in range(KC)]
    for t in range(TILES):
        for f in range(FC):
            j = t * FC + f
            order.append(("h", j))
            if f >= LAG_B:
                last = f == FC - 1
                if last and t + 1 < TILES:
                    order += [("xt", (TILES + t + 1) * KC + k) for k in range(KC)]
                order.append(("f", j - LAG_B))
                if last:
                    order.append(("f", j - LAG_B + 1))
            elif t > 0 and f < LAG_B - 1:
                order.append(("f", j - LAG_B + 1))
    order += [("f", TILES * FC - LAG_B + 1 + n) for n in range(LAG_B - 1)]
    return order


def xattn_ffn(nc, x, ctx_768, wq, bq, wk, bk, wv, bv, wo, bo, w1, b1, phases, w_real, w_imag, w2, b2,
              out, x1_dram, v_dram, u_dram):
    x_rows = x.rearrange("b (t n p) c -> (b t) p n c", n=NB, p=P)
    x1_rows = x1_dram.rearrange("(t n p) c -> t p n c", n=NB, p=P)
    out_rows = out.rearrange("b (t n p) c -> (b t) p n c", n=NB, p=P)

    stack = ExitStack()
    with stack:
        def sem(name):
            return stack.enter_context(nc.semaphore(name))

        def sems(name, n):
            return [sem(f"{name}{i}") for i in range(n)]

        def sbuf(where, name, shape, dt=F32):
            return where.enter_context(nc.sbuf_tensor(name, shape, dt))

        ident = sbuf(stack, "ident", [P, P])
        ones = sbuf(stack, "ones", [P, 1])
        stage = sbuf(stack, "stage", [P, STAGE, C])
        bo_row = sbuf(stack, "bo_row", [P, C])
        shift_rows = sbuf(stack, "shift_rows", [P, 2, NB])
        x_sb = [sbuf(stack, f"x_sb{i}", [P, NB, C]) for i in range(XBUFS)]
        xt_hi = sbuf(stack, "xt_hi", [P, KC, TOK], F32R)
        xt_lo = sbuf(stack, "xt_lo", [P, KC, TOK], F32R)
        stats = sbuf(stack, "stats", [P, 2, NB, 6])
        mv = sbuf(stack, "mv", [P, 2, NB, 2])
        var_eps = sbuf(stack, "var_eps", [P, 2, NB])
        rstd = sbuf(stack, "rstd", [P, 2, NB])
        minus_half = sbuf(stack, "minus_half", [P, NB])
        bq_sb = sbuf(stack, "bq_sb", [P, KC])
        bk_sb = sbuf(stack, "bk_sb", [P, KC])
        par = sbuf(stack, "par", [P, 4, FC])
        red = sbuf(stack, "red", [P, 8, FC])
        u_shift = sbuf(stack, "u_shift", [P, FC])
        gain = sbuf(stack, "gain", [P, FC])
        squares = sbuf(stack, "squares", [P, 2 * GROUPS])
        not_nan = sbuf(stack, "not_nan", [P, 2 * GROUPS])
        row_ok = sbuf(stack, "row_ok", [P, 1])
        ok_count = sbuf(stack, "ok_count", [1, 1], I32)

        start = ExitStack()
        wk_sb = sbuf(start, "wk_sb", [P, KK, C])
        wv_sb = sbuf(start, "wv_sb", [P, KK, C])
        ctxt = sbuf(start, "ctxt", [P, KK, B * KEYS])
        bv_row = sbuf(start, "bv_row", [P, C])
        first = ExitStack()
        ctx_sb = sbuf(first, "ctx_sb", [P, B // 2, CK])
        first.close()
        v_sb = sbuf(start, "v_sb", [P, B // 2, C])
        start.close()
        assert 2 * KK * C + KK * B * KEYS + C + (B // 2) * C <= 2 * HALF1 * C
        w1a_hi = sbuf(stack, "w1a_hi", [P, HALF1, KC, P], F32R)
        w1a_lo = sbuf(stack, "w1a_lo", [P, HALF1, KC, P], F32R)

        pa = ExitStack()
        wq_hi = sbuf(pa, "wq_hi", [P, KC, C], F32R)
        wq_lo = sbuf(pa, "wq_lo", [P, KC, C], F32R)
        kt = sbuf(pa, "kt", [P, KC, B * KEYS])
        k_masked = sbuf(pa, "k_masked", [P, HG, KEYS])
        kbd_hi = sbuf(pa, "kbd_hi", [P, KC, SG], F32R)
        kbd_lo = sbuf(pa, "kbd_lo", [P, KC, SG], F32R)
        v_mean = sbuf(pa, "v_mean", [P, KC, B])
        pick = sbuf(pa, "pick", [P, 2])
        mask_k = sbuf(pa, "mask_k", [P, HG])
        q_hi = sbuf(pa, "q_hi", [P, 2, TOK], F32R)
        q_lo = sbuf(pa, "q_lo", [P, 2, TOK], F32R)
        EARLY = 2 * KC * C + KC * B * KEYS + HG * KEYS + 2 * KC * SG + 2 * 2 * TOK
        q_full = sbuf(pa, "q_full", [P, TOK])
        v_in = sbuf(pa, "v_in", [P, 2, C])
        v_masked = sbuf(pa, "v_masked", [P, PAIRS, P])
        vbd_hi = sbuf(pa, "vbd_hi", [P, KC, PAIRS, P], F32R)
        vbd_lo = sbuf(pa, "vbd_lo", [P, KC, PAIRS, P], F32R)
        mask_v = sbuf(pa, "mask_v", [P, PAIRS, P])
        prob = sbuf(pa, "prob", [P, SCORE_BUFS, NB * HG, KEYS])
        halves = sbuf(pa, "halves", [P, NB * HG, KEYS // 2])
        top = sbuf(pa, "top", [P, 2, NB * HG])
        total = sbuf(pa, "total", [P, 2, NB * HG])
        inv = sbuf(pa, "inv", [P, 2, NB * HG])
        pt_hi = sbuf(pa, "pt_hi", [P, PAIRS, TOK], F32R)
        pt_lo = sbuf(pa, "pt_lo", [P, PAIRS, TOK], F32R)
        o_hi = sbuf(pa, "o_hi", [P, O_BUFS, TOK], F32R)
        o_lo = sbuf(pa, "o_lo", [P, O_BUFS, TOK], F32R)
        wo_hi = sbuf(pa, "wo_hi", [P, KC, C], F32R)
        wo_lo = sbuf(pa, "wo_lo", [P, KC, C], F32R)
        res = sbuf(pa, "res", [P, NB, C])
        u_sb = sbuf(pa, "u_sb", [B, C])
        vm_hi, vm_lo = (o[:, O_BUFS - 1, :].rearrange("p (k r b) -> p k r b", k=KC, b=B) for o in (o_hi, o_lo))
        pa.close()

        pb = ExitStack()
        turns = sbuf(pb, "turns", [P, 2, TOK])
        frac = sbuf(pb, "frac", [P, 2, TOK])
        hid = sbuf(pb, "hid", [P, 2, TOK])
        act_hi = sbuf(pb, "act_hi", [P, ACTS, TOK], F32R)
        act_lo = sbuf(pb, "act_lo", [P, ACTS, TOK], F32R)
        b2_row = sbuf(pb, "b2_row", [P, C])
        xn = sbuf(pb, "xn", [P, NB, C])
        assert (3 * 2 + 2 * ACTS) * TOK + C + NB * C <= EARLY
        w1b_hi = sbuf(pb, "w1b_hi", [P, FC - HALF1, KC, P], F32R)
        w1b_lo = sbuf(pb, "w1b_lo", [P, FC - HALF1, KC, P], F32R)
        w2_hi = sbuf(pb, "w2_hi", [P, FC, C], F32R)
        w2_lo = sbuf(pb, "w2_lo", [P, FC, C], F32R)
        pb.close()

        psum = stack.enter_context(nc.psum_tensor("psum", [P, BANKS, BANK], F32))

        order_a, order_b = plan_phase_a(), plan_phase_b()
        S_BANKS = NB * SG // BANK
        RING_A, RING_B = list(range(S_BANKS, BANKS)), list(range(NB))
        KT0_BANK = BANKS - 1
        Y_BANK = NB
        bank_of, before, held = {}, {}, {}

        def go_round(items, ring, kinds):
            for n, item in enumerate(it for it in items if it[0] in kinds):
                bank_of[item] = ring[n % len(ring)]
                before[item] = held.get(bank_of[item])
                held[bank_of[item]] = item

        held.update({n: ("s", GROUPS - 1) for n in range(S_BANKS)})
        go_round(order_a, RING_A, ("xt", "q", "v", "k", "m", "u", "pt", "o", "y"))
        go_round(order_b, RING_B, ("xt", "h"))

        def bank(item):
            return psum[:, bank_of[item], :]

        const_ready = sem("const_ready")
        bq_in = sem("bq_in")
        ctx_in, kw_in, vw_in, bias_in, par_in, b2_in = (sem(n) for n in (
            "ctx_in", "kw_in", "vw_in", "bias_in", "par_in", "b2_in"))
        ctxt_psum, ctxt_done = sem("ctxt_psum"), sem("ctxt_done")
        kt_psum, kt_done = sem("kt_psum"), sem("kt_done")
        kt0_psum, kt0_done = sem("kt0_psum"), sem("kt0_done")
        vn_psum, vn_done, vn_stored = sem("vn_psum"), sem("vn_done"), sem("vn_stored")
        bq_scaled = sem("bq_scaled")
        vm_psum, vm_done, vm_hi_done, vm_lo_done = (sem(n) for n in ("vm_psum", "vm_done", "vm_hi_done", "vm_lo_done"))
        u_psum, u_done, u_stored = sem("u_psum"), sem("u_done"), sem("u_stored")
        par_step, par_sin = sem("par_step"), sem("par_sin")
        x_in = sems("x_in", XBUFS)
        x0_in = sems("x0_in", NB)
        res_in, x1_stored = sems("res_in", NB), sems("x1_stored", NB)
        out_stored, last_stored = sems("out_stored", XBUFS), sem("last_stored")
        wqo_in = sems("wqo_in", 2 * KC)
        stage_in = sems("stage_in", STAGE)
        w_hi_done, w_lo_done = sem("w_hi_done"), sem("w_lo_done")
        v_dma = sems("v_dma", 2)
        stats_done, eps_done, rstd_done, xn_done = (sem(n) for n in ("stats_done", "eps_done", "rstd_done", "xn_done"))
        stats_raw, shift_rows_done, xn_half = sem("stats_raw"), sem("shift_rows_done"), sem("xn_half")
        q_full_done, halves_done = sem("q_full_done"), sem("halves_done")
        xn0_done = sem("xn0_done")
        x_biased, x1_whole = sem("x_biased"), sem("x1_whole")
        xt_psum, xt_hi_done, xt_lo_done = sem("xt_psum"), sem("xt_hi_done"), sem("xt_lo_done")
        q_psum, q_hi_done, q_lo_done = sem("q_psum"), sem("q_hi_done"), sem("q_lo_done")
        k_masked_done, kbd_hi_done, kbd_lo_done = sem("k_masked_done"), sem("kbd_hi_done"), sem("kbd_lo_done")
        v_masked_done, vbd_hi_done, vbd_lo_done = sem("v_masked_done"), sem("vbd_hi_done"), sem("vbd_lo_done")
        s_psum, clip_done, square_done = sem("s_psum"), sem("clip_done"), sem("square_done")
        top_done, shift_done, exp_done = sem("top_done"), sem("shift_done"), sem("exp_done")
        total_done, inv_done, prob_done = sem("total_done"), sem("inv_done"), sem("prob_done")
        pt_psum, pt_hi_done, pt_lo_done = sem("pt_psum"), sem("pt_hi_done"), sem("pt_lo_done")
        o_psum, o_hi_done, o_lo_done = sem("o_psum"), sem("o_hi_done"), sem("o_lo_done")
        y_psum, y_done = sem("y_psum"), sem("y_done")
        nan_step, nan_psum, nan_count = (sem(n) for n in ("nan_step", "nan_psum", "nan_count"))
        guard_done, last_done = sem("guard_done"), sem("last_done")
        fix_in, fix_add, fix_out = sem("fix_in"), sem("fix_add"), sem("fix_out")
        h_psum, turns_done, hid_done = sem("h_psum"), sem("turns_done"), sem("hid_done")
        whole_done, frac_done, sin_done = sem("whole_done"), sem("frac_done"), sem("sin_done")
        wave_done, act_hi_done, act_lo_done = sem("wave_done"), sem("act_hi_done"), sem("act_lo_done")
        f_psum, y2_done = sem("f_psum"), sem("y2_done")
        rows_psum = sem("rows_psum")

        freed_by = {"xt": xt_lo_done, "q": q_full_done, "pt": pt_lo_done, "o": o_lo_done, "y": y_done, "h": hid_done,
                    "v": vn_done, "k": kt_done, "m": vm_done, "u": u_done, "s": square_done}
        ups = {"s": S_BANKS}

        chunks = [(wq[k * P:(k + 1) * P, :], wq_hi[:, k, :], wq_lo[:, k, :], SCALE) for k in range(KC)]
        chunks += [(wo[k * P:(k + 1) * P, :], wo_hi[:, k, :], wo_lo[:, k, :], 1.0) for k in range(KC)]
        UNSTAGED = len(chunks)
        raw_q = prob[:].rearrange("p s h k -> p (s h k)")
        chunks += [(w1[f], w1a_hi[:, f], w1a_lo[:, f], 1.0) for f in range(HALF1)]
        CHUNKS_A = len(chunks)
        w2_chunk, w1_chunk = {}, {f: 2 * KC + f for f in range(HALF1)}
        for f in range(FC):
            w2_chunk[f] = len(chunks)
            chunks.append((w2[f * P:(f + 1) * P, :], w2_hi[:, f, :], w2_lo[:, f, :], 1.0))
            if f < FC - HALF1:
                w1_chunk[HALF1 + f] = len(chunks)
                chunks.append((w1[HALF1 + f], w1b_hi[:, f], w1b_lo[:, f], 1.0))

        def staged(c):
            if c < KC:
                return raw_q[:, c * C:(c + 1) * C], wqo_in[c], 16
            if c < UNSTAGED:
                return res[:, c - KC, :], wqo_in[c], 16
            n = c - UNSTAGED
            return stage[:, n % STAGE, :], stage_in[n % STAGE], 16 * (n // STAGE + 1)

        def like(flat, ap):
            return flat.rearrange("p (k m) -> p k m", m=P) if len(ap.shape) == 3 else flat

        def split_hi(act, need, c):
            raw, loaded, value = staged(c)
            _, hi, _, scale = chunks[c]
            need(loaded, value)
            act.activation(hi, like(raw, hi), ACT.Copy, scale=scale).then_inc(w_hi_done, 1)

        def split_lo(dve, need, c):
            raw, loaded, value = staged(c)
            _, hi, lo, scale = chunks[c]
            need(loaded, value)
            need(w_hi_done, c + 1)
            dve.scalar_tensor_tensor(out=lo, in0=like(raw, lo), scalar=scale, in1=hi.bitcast(F32), op0=ALU.mult,
                                     op1=ALU.subtract).then_inc(w_lo_done, 1)

        def x_tile(T):
            return x_sb[T % XBUFS], x_in[T % XBUFS], 16 * ((T + 1) // XBUFS)

        def normalised(T):
            return x_sb[T % XBUFS] if T < TILES else xn

        def load_values(queue, need, b):
            need(vn_stored, 16 * (b // 2 + 1))
            if b >= 2:
                need(v_masked_done, KC * (b - 1))
            for half in range(2):
                queue.dma_start(v_in[half * KEYS:(half + 1) * KEYS, b % 2, :], v_dram[b]).then_inc(v_dma[b % 2], 16)

        def later_chunks(j):
            return range(min(CHUNKS_A + STAGE * j, len(chunks)), min(CHUNKS_A + STAGE * (j + 1), len(chunks)))

        def phase_a_over(need):
            for blk in range(NB):
                need(x1_stored[blk], 16 * TILES)
            need(u_stored, 16)
            need(last_done, 1)

        def layer_norm_slot(i):
            if i == 0:
                return [(1, n) for n in range(NB)]
            T, n = divmod(i + 2 * KC, KC)
            return [(T, m) for m in range(0 if i == 1 else n, n + 1)] if T < TILES else []

        def scaled_norm(i):
            if i == 1:
                return 1
            T, at = divmod(i + KC, KC)
            return T if at == 0 and 1 < T < TILES else None

        def next_keys(i):
            b, at = divmod(i + KC, GB)
            return (b, at) if at < KC and 0 < b < B else None

        def next_values(i):
            b, at = divmod(i if i >= GB else i - 1, GB)
            return (b, at) if at < KC and 0 <= b < B else None

        def blocks_of(part):
            return range(part * NB // 2, (part + 1) * NB // 2)

        def residual(dve, need, t):
            tile = x_sb[t % XBUFS]
            for n in range(NB):
                need(x_biased, NB * t + n + 1)
                if n < NB - 1:
                    need(rows_psum, (NB - 1) * t + n + 1)
                else:
                    need(f_psum, FC * (t + 1))
                dve.tensor_tensor(tile[:, n, :], psum[:, Y_BANK + n, :], tile[:, n, :], ALU.add).then_inc(y2_done, 1)

        block = stack.enter_context(nc.Block())

        @block.sync
        def _(sp):
            need = Waits(sp)

            def load_x(t):
                if t >= XBUFS:
                    need(xt_psum, KC * (t - XBUFS + 1))
                sp.dma_start(x_sb[t % XBUFS][:], x_rows[t]).then_inc(x_in[t % XBUFS], 16)

            def load_chunk(c):
                raw, loaded, _ = staged(c)
                if c >= UNSTAGED + STAGE:
                    need(w_lo_done, c - STAGE + 1)
                sp.dma_start(like(raw, chunks[c][1]), chunks[c][0]).then_inc(loaded, 16)

            def load_res(n):
                t, blk = divmod(n, NB)
                if n >= NB:
                    need(x1_stored[blk], 16 * (n // NB))
                else:
                    need(w_lo_done, UNSTAGED)
                sp.dma_start(res[:, blk, :], x_rows[t][:, blk, :]).then_inc(res_in[blk], 16)

            for blk in range(NB):
                sp.dma_start(x_sb[0][:, blk, :], x_rows[0][:, blk, :]).then_inc(x0_in[blk], 16)
            sp.dma_start(ctx_sb[:], ctx_768.rearrange("(n b) k c -> (b k) n c", b=2)).then_inc(ctx_in, 16)
            sp.dma_start(wk_sb[:], wk.rearrange("(k p) c -> p k c", p=P)).then_inc(kw_in, 16)
            for c in range(KC):
                load_chunk(c)
            sp.dma_start(wv_sb[:], wv.rearrange("(k p) c -> p k c", p=P)).then_inc(vw_in, 16)
            for c in range(KC, 2 * KC):
                load_chunk(c)
            load_x(1)

            def store_values(n):
                need(vn_done, n + 1)
                sp.dma_start(v_dram[2 * n:2 * n + 2].rearrange("b k c -> (b k) c"), v_sb[:, n, :])\
                    .then_inc(vn_stored, 16)

            store_values(0)
            for b in range(2):
                load_values(sp, need, b)
            for c in range(UNSTAGED, UNSTAGED + STAGE):
                load_chunk(c)
            for t in range(2, 4):
                load_x(t)
            for n in range(1, B // 2):
                store_values(n)
            for n in range(NB):
                load_res(n)
            need(u_done, 1)
            sp.dma_start(u_dram, u_sb[:]).then_inc(u_stored, 16)
            for n in range(TILES * NB):
                t, blk = divmod(n, NB)
                need(y_done, n + 1)
                sp.dma_start(x1_rows[t][:, blk, :], res[:, blk, :]).then_inc(x1_stored[blk], 16)
                if 0 < n < TILES * NB - NB + 1:
                    load_res(n + NB - 1)
                if blk == 1 and t + 4 < TILES:
                    load_x(t + 4)
                if blk == 2 and t % TPB == 0 and t // TPB + 2 < B:
                    load_values(sp, need, t // TPB + 2)
                if blk == NB - 1 and UNSTAGED + STAGE + t < CHUNKS_A + STAGE:
                    load_chunk(UNSTAGED + STAGE + t)
                if n == NB * GUARDED + 1:
                    need(guard_done, 1)
                    need(xt_psum, KC * TILES)
                    for T in range(TILES, TILES + XBUFS):
                        tile, loaded, _ = x_tile(T)
                        sp.dma_start(tile[:], x1_rows[T - TILES]).then_inc(loaded, 16)

            need(s_psum, S_BANKS * GROUPS)
            sp.dma_start(b2_row[:], b2.partition_broadcast(P)).then_inc(b2_in, 16)
            for c in range(CHUNKS_A + STAGE, len(chunks)):
                load_chunk(c)
            for t in range(TILES):
                slot = t % XBUFS
                for blk in range(NB if t == TILES - 1 else 0):
                    need(y2_done, NB * t + blk + 1)
                    sp.dma_start(out_rows[t][:, blk, :], x_sb[slot][:, blk, :]).then_inc(last_stored, 16)
                if t == TILES - 1:
                    break
                need(y2_done, NB * (t + 1))
                sp.dma_start(out_rows[t], x_sb[slot][:]).then_inc(out_stored[slot], 16)
                if t + XBUFS < TILES:
                    need(out_stored[slot], 16 * (t // XBUFS + 1))
                    if t + XBUFS >= GUARDED:
                        need(last_done, 1)
                    sp.dma_start(x_sb[slot][:], x1_rows[t + XBUFS]).then_inc(x_in[slot], 16)
            for slot in range(XBUFS):
                need(out_stored[slot], 16 * len(range(slot, TILES - 1, XBUFS)))
            need(last_stored, 16 * NB)
            need(u_stored, 16)

        @block.gpsimd
        def _(pool):
            need = Waits(pool)
            made = 0

            def const(instruction):
                nonlocal made
                made += 1
                instruction.then_inc(const_ready, 1)
                need(const_ready, made)

            const(pool.memset(ident[:], 0.0))
            const(pool.memset(minus_half[:], -0.5))
            const(pool.memset(mask_k[:], 1.0))
            const(pool.memset(mask_v[:], 1.0))
            const(pool.memset(ones[:], 1.0))
            const(pool.memset(pick[:], 1.0 / KEYS))
            const(pool.affine_select(out=ident[:], in_=ident[:], compare_op=ALU.not_equal, fill=1.0, base=0,
                                     pattern=[[-1, P]], channel_multiplier=1))
            const(pool.affine_select(out=mask_k[:], in_=mask_k[:], compare_op=ALU.is_ge, fill=0.0, base=0,
                                     pattern=[[-D, HG]], channel_multiplier=1))
            for half in range(2):
                rows = slice(half * KEYS, (half + 1) * KEYS)
                const(pool.affine_select(out=mask_v[rows], in_=mask_v[rows], compare_op=ALU.is_ge, fill=0.0,
                                         base=-D * half, pattern=[[-2 * D, PAIRS], [1, P]], channel_multiplier=0))
                const(pool.memset(pick[rows, 1 - half:2 - half], 0.0))
            const(pool.affine_select(out=mask_k[:], in_=mask_k[:], compare_op=ALU.is_ge, fill=0.0, base=D - 1,
                                     pattern=[[D, HG]], channel_multiplier=-1))
            for half in range(2):
                rows = slice(half * KEYS, (half + 1) * KEYS)
                const(pool.affine_select(out=mask_v[rows], in_=mask_v[rows], compare_op=ALU.is_ge, fill=0.0,
                                         base=D * half + D - 1, pattern=[[2 * D, PAIRS], [-1, P]],
                                         channel_multiplier=0))
            assert made == CONSTS

            def rsqrt(T):
                need(eps_done, T + 1)
                if T >= 2:
                    need(xn_done, T - 1)
                need(const_ready, CONSTS)
                pool.tensor_tensor(rstd[:, T % 2, :], var_eps[:, T % 2, :], minus_half[:], ALU.pow)\
                    .then_inc(rstd_done, 1)

            def add_output_bias(t, n):
                tile, loaded, value = x_tile(TILES + t)
                need(loaded, value)
                need(bias_in, 48)
                pool.tensor_tensor(tile[:, n, :], tile[:, n, :], bo_row[:], ALU.add).then_inc(x1_whole, 1)

            def add_last_bias(t, n):
                tile, loaded, value = x_tile(TILES + t)
                need(xn_done, TILES + t + 1)
                need(x1_whole, NB * t + n + 1)
                need(b2_in, 16)
                pool.tensor_tensor(tile[:, n, :], tile[:, n, :], b2_row[:], ALU.add).then_inc(x_biased, 1)

            def mask_keys(b, g):
                n = b * KC + g
                if b:
                    need(kt_done, KC)
                else:
                    need(kt0_done, g + 1)
                if n:
                    need(kbd_lo_done, n)
                keys = kt[:, g, b * KEYS:(b + 1) * KEYS]
                pool.tensor_tensor(k_masked[:], keys.unsqueeze(1).to_broadcast([P, HG, KEYS]),
                                   mask_k[:].unsqueeze(2).to_broadcast([P, HG, KEYS]), ALU.mult)\
                    .then_inc(k_masked_done, 1)

            def mask_values(b, g):
                n = b * KC + g
                need(v_dma[b % 2], 32 * (b // 2 + 1))
                if n:
                    need(vbd_lo_done, n)
                values = v_in[:, b % 2, g * P:(g + 1) * P]
                pool.tensor_tensor(v_masked[:], values.unsqueeze(1).to_broadcast([P, PAIRS, P]), mask_v[:], ALU.mult)\
                    .then_inc(v_masked_done, 1)

            def q_to_lo(i):
                need(q_hi_done, i + 1)
                pool.tensor_tensor(q_lo[:, i % 2, :], q_full[:], q_hi[:, i % 2, :].bitcast(F32), ALU.subtract)\
                    .then_inc(q_lo_done, 1)

            def add_halves(i):
                need(exp_done, i + 1)
                if i:
                    need(total_done, i)
                rows = prob[:, i % SCORE_BUFS]
                pool.tensor_tensor(halves[:], rows[:, :, 0:KEYS // 2], rows[:, :, KEYS // 2:KEYS], ALU.add)\
                    .then_inc(halves_done, 1)

            def shift(i):
                need(top_done, i + 1)
                rows = prob[:, i % SCORE_BUFS]
                pool.tensor_tensor(rows, rows, top[:, i % 2, :].unsqueeze(2).to_broadcast([P, NB * HG, KEYS]),
                                   ALU.subtract).then_inc(shift_done, 1)

            def normalise(i):
                need(inv_done, i + 1)
                rows = prob[:, i % SCORE_BUFS]
                pool.tensor_tensor(rows, rows, inv[:, i % 2, :].unsqueeze(2).to_broadcast([P, NB * HG, KEYS]),
                                   ALU.mult).then_inc(prob_done, 1)

            rsqrt(0)
            mask_keys(0, 0)
            q_to_lo(0)
            for i in range(GROUPS + 1):
                t, g = divmod(i, KC)
                if i:
                    add_halves(i - 1)
                if scaled_norm(i):
                    rsqrt(scaled_norm(i))
                if i + 1 < KC:
                    mask_keys(0, i + 1)
                if next_keys(i - 1):
                    mask_keys(*next_keys(i - 1))
                if next_values(i - 1):
                    mask_values(*next_values(i - 1))
                if i:
                    normalise(i - 1)
                if i < GROUPS:
                    shift(i)
                if i + 1 < GROUPS:
                    q_to_lo(i + 1)

            need(nan_count, 1)
            count = pool.alloc_register("rows_without_nan")
            pool.reg_load(count, ok_count[0:1, 0:1])

            def uniform(n, rows, tile, u_row, b):
                if n:
                    pool.wait_ge(fix_out, 16 * n)
                pool.dma_start(tile, rows(x_rows)).then_inc(fix_in, 16)
                pool.dma_start(u_row, u_dram[b].partition_broadcast(P)).then_inc(fix_in, 16)
                pool.wait_ge(fix_in, 32 * (n + 1))
                pool.tensor_tensor(tile, tile, u_row.unsqueeze(1).to_broadcast([P, tile.shape[1], C]), ALU.add)\
                    .then_inc(fix_add, 1)
                pool.wait_ge(fix_add, n + 1)
                pool.dma_start(rows(x1_rows), tile).then_inc(fix_out, 16)

            with pool.If_ne(count, P):
                pool.wait_ge(xt_psum, KC * TILES)
                pool.wait_ge(u_stored, 16)
                for blk in range(NB):
                    pool.wait_ge(x1_stored[blk], 16 * GUARDED)
                for t in range(GUARDED):
                    uniform(t, lambda x: x[t], x_sb[0][:], x_sb[1][:, 0, :], t // TPB)
                pool.wait_ge(fix_out, 16 * GUARDED)
            pool.memset(ones[:], 1.0).then_inc(guard_done, 1)

            for n in range(NB):
                add_output_bias(0, n)
            rsqrt(TILES)

            with pool.If_ne(count, P):
                for blk in range(NB):
                    pool.wait_ge(x1_stored[blk], 16 * TILES)
                for m in range((TILES - GUARDED) * NB):
                    t, blk = GUARDED + m // NB, m % NB
                    uniform(GUARDED + m, lambda x: x[t][:, blk:blk + 1, :], q_full[:].unsqueeze(1),
                            halves[:].rearrange("p h k -> p (h k)"), t // TPB)
                pool.wait_ge(fix_out, 16 * (GUARDED + (TILES - GUARDED) * NB))
            pool.memset(ones[:], 1.0).then_inc(last_done, 1)

            for n in range(NB):
                add_last_bias(0, n)
            for t in range(TILES):
                for f in range(FC):
                    j = t * FC + f
                    need(whole_done, j + 1)
                    pool.tensor_tensor(frac[:, j % 2, :], turns[:, j % 2, :], frac[:, j % 2, :], ALU.subtract)\
                        .then_inc(frac_done, 1)
                    if t + 1 < TILES:
                        if f in (LN_AT, LN_AT + 1):
                            for n in blocks_of(f - LN_AT):
                                add_output_bias(t + 1, n)
                        if f == LN_AT + 3:
                            rsqrt(TILES + t + 1)
                        if f in (LN_AT + 6, LN_AT + 7):
                            for n in blocks_of(f - LN_AT - 6):
                                add_last_bias(t + 1, n)

        @block.scalar
        def _(act):
            need = Waits(act)
            act.dma_start(bq_sb[:], bq).then_inc(bq_in, 16)
            act.dma_start(bk_sb[:], bk).then_inc(bias_in, 16)
            for dst, src in ((bv_row, bv), (bo_row, bo)):
                act.dma_start(dst[:], src.partition_broadcast(P)).then_inc(bias_in, 16)
            for n, vector in enumerate((phases, w_real, w_imag, b1)):
                act.dma_start(par[:, n, :], vector).then_inc(par_in, 16)

            def param_sines():
                need(par_step, PAR_REDUCED)
                act.activation(red[:, 5, :], red[:, 3, :], ACT.Sin)
                act.activation(red[:, 6, :], red[:, 4, :], ACT.Sin).then_inc(par_sin, 1)

            def xt_to_hi(n):
                T, k = divmod(n, KC)
                need(xt_psum, n + 1)
                if 0 < T < TILES:
                    need(q_psum, KC * T)
                elif T == TILES:
                    need(q_psum, GROUPS)
                elif T > TILES:
                    need(h_psum, FC * (T - TILES))
                act.activation(xt_hi[:, k, :], bank(("xt", n)), ACT.Copy).then_inc(xt_hi_done, 1)

            def layer_rows(T, blocks):
                tile, loaded, value = x_tile(T)
                need(loaded, value)
                need(shift_rows_done, T + 1)
                if T == TILES:
                    need(s_psum, S_BANKS * GROUPS)
                if T > TILES:
                    need(xt_psum, KC * T)
                for n in blocks:
                    last = act.activation(normalised(T)[:, n, :], tile[:, n, :], ACT.Identity,
                                          bias=shift_rows[:, T % 2, n:n + 1], scale=rstd[:, T % 2, n:n + 1])
                last.then_inc(xn_done if NB - 1 in blocks or T == 0 else xn_half, 1)

            def q_to_hi(i):
                need(q_psum, i + 1)
                need(bq_scaled, 1)
                if i:
                    need(q_lo_done, i)
                act.activation(q_full[:], bank(("q", i)), ACT.Identity, bias=bq_sb[:, i % KC:i % KC + 1])\
                    .then_inc(q_full_done, 1)
                if i >= 2:
                    need(s_psum, S_BANKS * (i - 1))
                need(q_full_done, i + 1)
                act.activation(q_hi[:, i % 2, :], q_full[:], ACT.Copy).then_inc(q_hi_done, 1)

            def keys_to_hi(b, g):
                need(k_masked_done, b * KC + g + 1)
                if b:
                    need(s_psum, S_BANKS * ((b - 1) * GB + GB - KC + g + 1))
                act.activation(kbd_hi[:, g, :], k_masked[:].rearrange("p h k -> p (h k)"), ACT.Copy)\
                    .then_inc(kbd_hi_done, 1)

            def values_to_hi(b, g):
                need(v_masked_done, b * KC + g + 1)
                if b:
                    need(o_psum, (b - 1) * GB + GB - KC + g + 1)
                act.activation(vbd_hi[:, g], v_masked[:], ACT.Copy).then_inc(vbd_hi_done, 1)

            need(bq_in, 16)
            act.activation(bq_sb[:], bq_sb[:], ACT.Copy, scale=SCALE).then_inc(bq_scaled, 1)
            need(x0_in[1], 16)
            layer_rows(0, blocks_of(0))
            for c in range(KC):
                split_hi(act, need, c)
            need(bias_in, 48)
            need(kt0_psum, KC)
            for g in range(KC):
                act.activation(kt[:, g, 0:KEYS], psum[:, KT0_BANK, g * KEYS:(g + 1) * KEYS], ACT.Identity,
                               bias=bk_sb[:, g:g + 1]).then_inc(kt0_done, 1)
            for k in range(KC):
                xt_to_hi(k)
            keys_to_hi(0, 0)
            q_to_hi(0)

            for i in range(GROUPS + LAG_A):
                t, g = divmod(i, KC)
                late = i - LAG_A
                if g == 1 and 1 < t + 1 < TILES:
                    layer_rows(t + 1, range(NB))
                if i < GROUPS:
                    for n in range(S_BANKS * i, S_BANKS * (i + 1)):
                        need(clip_done, n + 1)
                        scores = psum[:, n % S_BANKS, :]
                        act.activation(scores, scores, ACT.Square, accum_out=squares[:, n:n + 1])\
                            .then_inc(square_done, 1)
                if late >= 0:
                    for n in range(late * PAIRS, (late + 1) * PAIRS):
                        need(pt_psum, n + 1)
                        need(o_psum, late)
                        act.activation(pt_hi[:, n % PAIRS, :], bank(("pt", n)), ACT.Copy).then_inc(pt_hi_done, 1)
                if i == 1:
                    layer_rows(1, range(NB))
                if i + 1 < KC:
                    keys_to_hi(0, i + 1)
                if next_keys(i - 1):
                    keys_to_hi(*next_keys(i - 1))
                if next_values(i - 1):
                    values_to_hi(*next_values(i - 1))
                if i + 1 < GROUPS:
                    q_to_hi(i + 1)
                if i < GROUPS:
                    need(shift_done, i + 1)
                    rows = prob[:, i % SCORE_BUFS]
                    act.activation(rows, rows, ACT.Exp).then_inc(exp_done, 1)
                for k in (range(2) if i == 0 else range(i + 1, i + 2) if i < KC - 1 else ()):
                    need(kt_psum, k + 1)
                    act.activation(kt[:, k, KEYS:], bank(("k", k))[:, KEYS:], ACT.Identity, bias=bk_sb[:, k:k + 1])\
                        .then_inc(kt_done, 1)
                if g == 2 and t + 1 < TILES:
                    for k in range(KC):
                        xt_to_hi((t + 1) * KC + k)
                if 1 <= i <= KC:
                    split_hi(act, need, KC + i - 1)
                if i == M_STEP + 1:
                    need(vm_done, 1)
                    act.activation(vm_hi, v_mean[:].unsqueeze(2).to_broadcast([P, KC, P // B, B]), ACT.Copy)\
                        .then_inc(vm_hi_done, 1)
                if g == KC - 1 and 1 <= t <= HALF1:
                    need(vm_psum, 1)
                    need(vn_stored, 16 * (B // 2))
                    split_hi(act, need, UNSTAGED + t - 1)
                if late >= 0:
                    need(o_psum, late + 1)
                    if late == O_BUFS - 1:
                        need(u_psum, 1)
                    if late >= O_BUFS:
                        need(y_psum, NB * ((late - O_BUFS) // KC + 1))
                    act.activation(o_hi[:, late % O_BUFS, :], bank(("o", late)), ACT.Copy).then_inc(o_hi_done, 1)

            param_sines()
            layer_rows(TILES, range(NB))
            for k in range(KC):
                xt_to_hi(TILES * KC + k)

            def finish(j):
                need(frac_done, j + 1)
                act.activation(frac[:, j % 2, :], frac[:, j % 2, :], ACT.Sin, scale=SIN_SCALE).then_inc(sin_done, 1)
                need(wave_done, j + 1)
                if j >= ACTS:
                    need(f_psum, j - ACTS + 1)
                act.activation(act_hi[:, j % ACTS, :], hid[:, j % 2, :], ACT.Relu).then_inc(act_hi_done, 1)

            need(s_psum, S_BANKS * GROUPS)
            for j in range(TILES * FC):
                t, f = divmod(j, FC)
                need(h_psum, j + 1)
                if j >= 2:
                    need(frac_done, j - 1)
                    need(act_lo_done, j - 1)
                act.activation(turns[:, j % 2, :], bank(("h", j)), ACT.Identity, bias=u_shift[:, f:f + 1],
                               scale=0.1 / TWO_PI).then_inc(turns_done, 1)
                act.activation(hid[:, j % 2, :], bank(("h", j)), ACT.Identity, bias=par[:, 3, f:f + 1])\
                    .then_inc(hid_done, 1)
                if f == FC - 1 and t + 1 < TILES:
                    for k in range(KC):
                        xt_to_hi((TILES + t + 1) * KC + k)
                if j:
                    finish(j - 1)
                if t + 1 < TILES and f in (LN_AT + 4, LN_AT + 5):
                    layer_rows(TILES + t + 1, blocks_of(f - LN_AT - 4))
                if j == 0:
                    phase_a_over(need)
                for c in later_chunks(j):
                    split_hi(act, need, c)
            finish(TILES * FC - 1)

        @block.vector
        def _(dve):
            need = Waits(dve)
            steps = 0

            def par_scalar(dst, src, *scalars_and_ops):
                nonlocal steps
                steps += 1
                dve.tensor_scalar(dst, src, *scalars_and_ops).then_inc(par_step, 1)
                need(par_step, steps)

            def par_tensor(dst, in0, scalar, in1, op0, op1):
                nonlocal steps
                steps += 1
                dve.scalar_tensor_tensor(out=dst, in0=in0, scalar=scalar, in1=in1, op0=op0, op1=op1)\
                    .then_inc(par_step, 1)
                need(par_step, steps)

            def layer_stats(T, blocks):
                tile, loaded, value = x_tile(T)
                need(loaded, value)
                if T >= 2:
                    need(shift_rows_done, T - 1)
                for n in blocks:
                    if T >= TILES:
                        need(x1_whole, NB * (T - TILES) + n + 1)
                    if T == 0:
                        need(x0_in[n], 16)
                    dve.bn_stats(stats[:, T % 2, n, :], tile[:, n, :]).then_inc(stats_raw, 1)
                if NB - 1 in blocks:
                    need(stats_raw, NB * (T + 1))
                    for n in range(NB):
                        last = dve.bn_aggr(mv[:, T % 2, n, :], stats[:, T % 2, n, :])
                    last.then_inc(stats_done, 1)
                    need(stats_done, T + 1)
                    dve.tensor_scalar(var_eps[:, T % 2, :], mv[:, T % 2, :, 1], EPS, None, ALU.add)\
                        .then_inc(eps_done, 1)

            def layer_shift(T):
                need(rstd_done, T + 1)
                dve.scalar_tensor_tensor(out=shift_rows[:, T % 2, :], in0=mv[:, T % 2, :, 0], scalar=-1.0,
                                         in1=rstd[:, T % 2, :], op0=ALU.mult, op1=ALU.mult)\
                    .then_inc(shift_rows_done, 1)

            def xt_to_lo(n):
                T, k = divmod(n, KC)
                need(xt_hi_done, n + 1)
                dve.tensor_tensor(xt_lo[:, k, :], bank(("xt", n)), xt_hi[:, k, :].bitcast(F32), ALU.subtract)\
                    .then_inc(xt_lo_done, 1)

            theta, w_re, w_im, bias1 = (par[:, n, :] for n in range(4))

            def phases_reduced():
                need(par_in, 64)

                def reduce_phase(dst, src, tmp):
                    par_scalar(tmp, src, 1.0 / TWO_PI, ROUND, ALU.mult, ALU.add)
                    par_scalar(tmp, tmp, ROUND, None, ALU.subtract)
                    par_tensor(dst, tmp, -PI_A, src, ALU.mult, ALU.add)
                    par_tensor(dst, tmp, -PI_B, dst, ALU.mult, ALU.add)
                    par_tensor(dst, tmp, -PI_C, dst, ALU.mult, ALU.add)

                reduce_phase(red[:, 1, :], theta, red[:, 0, :])
                par_scalar(red[:, 2, :], red[:, 1, :], math.pi / 2, None, ALU.add)
                reduce_phase(red[:, 7, :], red[:, 2, :], red[:, 0, :])
                pi_down = 3.1415925
                par_scalar(red[:, 3, :], red[:, 1, :], pi_down, -pi_down, ALU.min, ALU.max)
                par_scalar(red[:, 4, :], red[:, 7, :], pi_down, -pi_down, ALU.min, ALU.max)
                assert steps == PAR_REDUCED
                par_tensor(red[:, 2, :], bias1, 0.1, red[:, 1, :], ALU.mult, ALU.add)
                par_scalar(u_shift[:], red[:, 2, :], 1.0 / TWO_PI, None, ALU.mult)

            def phases_gain():
                need(par_sin, 1)
                par_tensor(red[:, 0, :], red[:, 6, :], 1.0, w_re, ALU.mult, ALU.mult)
                par_tensor(red[:, 2, :], red[:, 5, :], 1.0, w_im, ALU.mult, ALU.mult)
                par_tensor(red[:, 0, :], red[:, 0, :], 1.0, red[:, 2, :], ALU.mult, ALU.add)
                par_tensor(gain[:], red[:, 0, :], 0.1, w_im, ALU.mult, ALU.mult)

            layer_stats(0, range(NB))
            layer_shift(0)
            need(shift_rows_done, 1)
            for n in blocks_of(1):
                last = dve.tensor_scalar(normalised(0)[:, n, :], x_sb[0][:, n, :], rstd[:, 0, n:n + 1],
                                         shift_rows[:, 0, n:n + 1], ALU.mult, ALU.add)
            last.then_inc(xn0_done, 1)
            for k in range(KK):
                need(ctxt_psum, k + 1)
                dve.tensor_copy(ctxt[:, k, :], psum[:, k, :]).then_inc(ctxt_done, 1)

            def keys_to_lo(b, g):
                need(kbd_hi_done, b * KC + g + 1)
                dve.tensor_tensor(kbd_lo[:, g, :], k_masked[:].rearrange("p h k -> p (h k)"),
                                  kbd_hi[:, g, :].bitcast(F32), ALU.subtract).then_inc(kbd_lo_done, 1)

            def values_to_lo(b, g):
                need(vbd_hi_done, b * KC + g + 1)
                dve.tensor_tensor(vbd_lo[:, g], v_masked[:], vbd_hi[:, g].bitcast(F32), ALU.subtract)\
                    .then_inc(vbd_lo_done, 1)

            def values_rows(n):
                need(vn_psum, n + 1)
                need(bias_in, 48)
                dve.tensor_tensor(v_sb[:, n, :], bank(("v", n)), bv_row[:], ALU.add).then_inc(vn_done, 1)

            def x1_block(n):
                blk = n % NB
                need(res_in[blk], 16 * (n // NB + 1))
                need(y_psum, n + 1)
                dve.tensor_tensor(res[:, blk, :], bank(("y", n)), res[:, blk, :], ALU.add).then_inc(y_done, 1)

            def o_to_lo(i):
                need(o_hi_done, i + 1)
                dve.tensor_tensor(o_lo[:, i % O_BUFS, :], bank(("o", i)), o_hi[:, i % O_BUFS, :].bitcast(F32),
                                  ALU.subtract).then_inc(o_lo_done, 1)

            for c in range(KC):
                split_lo(dve, need, c)
            for k in range(KC):
                xt_to_lo(k)
            keys_to_lo(0, 0)
            values_rows(0)

            for i in range(STEPS_A):
                t, g = divmod(i, KC)
                late = i - LAG_A
                if 1 <= late <= GROUPS:
                    o_to_lo(late - 1)
                if 1 <= i <= GROUPS:
                    need(halves_done, i)
                    if i >= 3:
                        need(prob_done, i - 2)
                    dve.reduce_sum(total[:, (i - 1) % 2, :], halves[:], AX_X).then_inc(total_done, 1)
                    need(total_done, i)
                    dve.reciprocal(inv[:, (i - 1) % 2, :], total[:, (i - 1) % 2, :]).then_inc(inv_done, 1)
                if i == GROUPS:
                    need(square_done, S_BANKS * GROUPS)
                    dve.tensor_tensor(not_nan[:], squares[:], squares[:], ALU.is_equal).then_inc(nan_step, 1)
                    need(nan_step, 1)
                    dve.tensor_reduce(row_ok[:], not_nan[:], AX_X, ALU.min).then_inc(nan_step, 1)
                if i < GROUPS:
                    if i >= SCORE_BUFS:
                        need(pt_psum, PAIRS * (i - SCORE_BUFS + 1))
                    for n in range(S_BANKS * i, S_BANKS * (i + 1)):
                        need(s_psum, n + 1)
                        half = n % S_BANKS
                        rows = NB * HG // S_BANKS
                        dve.tensor_scalar(prob[:, i % SCORE_BUFS, half * rows:(half + 1) * rows, :]
                                          .rearrange("p h k -> p (h k)"), psum[:, half, :], CLAMP, -CLAMP,
                                          ALU.min, ALU.max).then_inc(clip_done, 1)
                    need(clip_done, S_BANKS * (i + 1))
                    if i >= 2:
                        need(shift_done, i - 1)
                    dve.reduce_max(top[:, i % 2, :], prob[:, i % SCORE_BUFS], AX_X).then_inc(top_done, 1)
                if scaled_norm(i):
                    layer_shift(scaled_norm(i))
                if 0 <= late < GROUPS:
                    for n in range(late * PAIRS, (late + 1) * PAIRS):
                        need(pt_hi_done, n + 1)
                        dve.tensor_tensor(pt_lo[:, n % PAIRS, :], bank(("pt", n)), pt_hi[:, n % PAIRS, :].bitcast(F32),
                                          ALU.subtract).then_inc(pt_lo_done, 1)
                if i + 1 < KC:
                    keys_to_lo(0, i + 1)
                if next_keys(i - 1):
                    keys_to_lo(*next_keys(i - 1))
                if next_values(i - 1):
                    values_to_lo(*next_values(i - 1))
                for T, n in layer_norm_slot(i):
                    layer_stats(T, range(n, n + 1))
                if g == 2 and t + 1 < TILES:
                    for k in range(KC):
                        xt_to_lo((t + 1) * KC + k)
                if 1 <= i < B // 2:
                    values_rows(i)
                if 1 <= i <= KC:
                    split_lo(dve, need, KC + i - 1)
                if i == M_STEP:
                    need(vm_psum, 1)
                    dve.tensor_copy(v_mean[:], bank(("m", 0))[:, 0:KC * B].rearrange("p (k b) -> p k b", b=B))\
                        .then_inc(vm_done, 1)
                if i == M_STEP + 1:
                    need(vm_hi_done, 1)
                    need(vm_done, 1)
                    dve.tensor_tensor(vm_lo, v_mean[:].unsqueeze(2).to_broadcast([P, KC, P // B, B]),
                                      vm_hi.bitcast(F32), ALU.subtract).then_inc(vm_lo_done, 1)
                if i == U_STEP:
                    need(u_psum, 1)
                    dve.tensor_copy(u_sb[:], bank(("u", 0))[0:B, :]).then_inc(u_done, 1)
                if g == KC - 1 and 1 <= t <= HALF1:
                    need(vm_psum, 1)
                    need(vn_stored, 16 * (B // 2))
                    split_lo(dve, need, UNSTAGED + t - 1)
                if i == 3 * KC + 1:
                    phases_reduced()
                if i == GROUPS:
                    need(nan_psum, 1)
                    dve.tensor_copy(ok_count[:], psum[0:1, 0, 0:1]).then_inc(nan_count, 1)
                if i in (STEPS_A - 3, STEPS_A - 2):
                    layer_stats(TILES, blocks_of(i - STEPS_A + 3))
                if i == STEPS_A - 1:
                    layer_shift(TILES)
                if output_block(i) is not None:
                    x1_block(output_block(i))

            for k in range(KC):
                xt_to_lo(TILES * KC + k)

            def finish(j):
                need(sin_done, j + 1)
                need(hid_done, j + 1)
                f = j % FC
                dve.scalar_tensor_tensor(out=hid[:, j % 2, :], in0=frac[:, j % 2, :], scalar=gain[:, f:f + 1],
                                         in1=hid[:, j % 2, :], op0=ALU.mult, op1=ALU.add).then_inc(wave_done, 1)
                need(act_hi_done, j + 1)
                dve.scalar_tensor_tensor(out=act_lo[:, j % ACTS, :], in0=hid[:, j % 2, :], scalar=0.0,
                                         in1=act_hi[:, j % ACTS, :].bitcast(F32), op0=ALU.max, op1=ALU.subtract)\
                    .then_inc(act_lo_done, 1)

            phases_gain()
            need(s_psum, S_BANKS * GROUPS)
            for j in range(TILES * FC):
                t, f = divmod(j, FC)
                if f == LAG_B - 1 and t > 0:
                    residual(dve, need, t - 1)
                need(turns_done, j + 1)
                if j >= 2:
                    need(wave_done, j - 1)
                dve.tensor_scalar(frac[:, j % 2, :], turns[:, j % 2, :], ROUND, ROUND, ALU.add, ALU.subtract)\
                    .then_inc(whole_done, 1)
                if f == FC - 1 and t + 1 < TILES:
                    for k in range(KC):
                        xt_to_lo((TILES + t + 1) * KC + k)
                if j:
                    finish(j - 1)
                if j == 0:
                    phase_a_over(need)
                for c in later_chunks(j):
                    split_lo(dve, need, c)
                if t + 1 < TILES and f in (LN_AT + 1, LN_AT + 2):
                    layer_stats(TILES + t + 1, blocks_of(f - LN_AT - 1))
                if t + 1 < TILES and f == LN_AT + 3:
                    layer_shift(TILES + t + 1)
            finish(TILES * FC - 1)
            residual(dve, need, TILES - 1)

        @block.tensor
        def _(pe):
            need = Waits(pe)

            def product(o, stationary, moving, first=True, last=True):
                (a_hi, a_lo), (b_hi, b_lo) = stationary, moving
                for n, (a, b_) in enumerate(((a_hi, b_hi), (a_hi, b_lo), (a_lo, b_hi))):
                    m = pe.matmul(o, a, b_, start=first and n == 0, stop=last and n == 2)
                return m

            def bank_free(item):
                prior = before[item]
                if prior:
                    need(freed_by[prior[0]], ups.get(prior[0], 1) * (prior[1] + 1))

            need(const_ready, CONSTS)
            need(ctx_in, 16)
            for k in range(KK):
                for n in range(B // 2):
                    m = pe.transpose(psum[:, k, n * P:(n + 1) * P], ctx_sb[:, n, k * P:(k + 1) * P], ident[:])
                m.then_inc(ctxt_psum, 1)
            need(ctxt_done, KK)

            def kt0(_):
                need(kw_in, 16)
                for g in range(KC):
                    for k in range(KK):
                        m = pe.matmul(psum[:, KT0_BANK, g * KEYS:(g + 1) * KEYS], wk_sb[:, k, g * P:(g + 1) * P],
                                      ctxt[:, k, 0:KEYS], start=k == 0, stop=k == KK - 1)
                    m.then_inc(kt0_psum, 1)

            def k_(g):
                bank_free(("k", g))
                for k in range(KK):
                    m = pe.matmul(bank(("k", g))[:, KEYS:], wk_sb[:, k, g * P:(g + 1) * P], ctxt[:, k, KEYS:],
                                  start=k == 0, stop=k == KK - 1)
                m.then_inc(kt_psum, 1)

            def v(n):
                need(vw_in, 16)
                if bank_of[("v", n)] == KT0_BANK:
                    need(kt0_done, KC)
                bank_free(("v", n))
                for k in range(KK):
                    m = pe.matmul(bank(("v", n)), ctxt[:, k, n * P:(n + 1) * P], wv_sb[:, k, :], start=k == 0,
                                  stop=k == KK - 1)
                m.then_inc(vn_psum, 1)

            def m_(_):
                need(vn_done, B // 2)
                bank_free(("m", 0))
                for n in range(B // 2):
                    for g in range(KC):
                        m = pe.matmul(bank(("m", 0))[:, g * B + 2 * n:g * B + 2 * n + 2], v_sb[:, n, g * P:(g + 1) * P],
                                      pick[:], start=True, stop=True)
                m.then_inc(vm_psum, 1)

            def u(_):
                need(vm_lo_done, 1)
                need(w_lo_done, 2 * KC)
                bank_free(("u", 0))
                for g in range(KC):
                    m = product(bank(("u", 0)), [mean[:, g].rearrange("p r b -> p (r b)") for mean in (vm_hi, vm_lo)],
                                (wo_hi[:, g, :], wo_lo[:, g, :]), g == 0, g == KC - 1)
                m.then_inc(u_psum, 1)

            def nan(_):
                need(nan_step, 2)
                pe.matmul(psum[0:1, 0, 0:1], row_ok[:], ones[:], start=True, stop=True).then_inc(nan_psum, 1)

            def xt(n):
                T, k = divmod(n, KC)
                need(xn_done, T + 1)
                need(xn0_done, 1)
                bank_free(("xt", n))
                for blk in range(NB):
                    m = pe.transpose(bank(("xt", n))[:, blk * P:(blk + 1) * P],
                                     normalised(T)[:, blk, k * P:(k + 1) * P], ident[:])
                m.then_inc(xt_psum, 1)

            def q(i):
                t, g = divmod(i, KC)
                need(w_lo_done, KC)
                bank_free(("q", i))
                for k in range(KC):
                    need(xt_lo_done, t * KC + k + 1)
                    cols = slice(g * P, (g + 1) * P)
                    m = product(bank(("q", i)), (wq_hi[:, k, cols], wq_lo[:, k, cols]),
                                (xt_hi[:, k, :], xt_lo[:, k, :]), k == 0, k == KC - 1)
                m.then_inc(q_psum, 1)

            def s(i):
                t, g = divmod(i, KC)
                need(q_lo_done, i + 1)
                need(kbd_lo_done, (t // TPB) * KC + g + 1)
                per_bank = BANK // SG
                for blk in range(NB):
                    half, at = divmod(blk, per_bank)
                    if i:
                        need(square_done, S_BANKS * (i - 1) + half + 1)
                    toks = slice(blk * P, (blk + 1) * P)
                    m = product(psum[:, half, at * SG:(at + 1) * SG], (q_hi[:, i % 2, toks], q_lo[:, i % 2, toks]),
                                (kbd_hi[:, g, :], kbd_lo[:, g, :]))
                    if at == per_bank - 1:
                        m.then_inc(s_psum, 1)

            def pt(n):
                i, j = divmod(n, PAIRS)
                need(prob_done, i + 1)
                bank_free(("pt", n))
                for blk in range(NB):
                    heads = slice(blk * HG + 2 * j, blk * HG + 2 * j + 2)
                    m = pe.transpose(bank(("pt", n))[:, blk * P:(blk + 1) * P],
                                     prob[:, i % SCORE_BUFS, heads, :].rearrange("p h k -> p (h k)"), ident[:])
                m.then_inc(pt_psum, 1)

            def o(i):
                t, g = divmod(i, KC)
                need(vbd_lo_done, (t // TPB) * KC + g + 1)
                bank_free(("o", i))
                for j in range(PAIRS):
                    need(pt_lo_done, PAIRS * i + j + 1)
                    m = product(bank(("o", i)), (vbd_hi[:, g, j, :], vbd_lo[:, g, j, :]),
                                (pt_hi[:, j, :], pt_lo[:, j, :]), j == 0, j == PAIRS - 1)
                m.then_inc(o_psum, 1)

            def y(n):
                t, blk = divmod(n, NB)
                need(w_lo_done, 2 * KC)
                bank_free(("y", n))
                toks = slice(blk * P, (blk + 1) * P)
                for g in range(KC):
                    need(o_lo_done, t * KC + g + 1)
                    slot = (t * KC + g) % O_BUFS
                    m = product(bank(("y", n)), (o_hi[:, slot, toks], o_lo[:, slot, toks]),
                                (wo_hi[:, g, :], wo_lo[:, g, :]), g == 0, g == KC - 1)
                m.then_inc(y_psum, 1)

            run = {"kt0": kt0, "k": k_, "v": v, "m": m_, "u": u, "xt": xt, "q": q, "s": s, "pt": pt, "o": o, "y": y,
                   "nan": nan}
            for kind, n in order_a:
                run[kind](n)

            def h(j):
                t, f = divmod(j, FC)
                need(w_lo_done, w1_chunk[f] + 1)
                bank_free(("h", j))
                hi, lo = (w1a_hi, w1a_lo) if f < HALF1 else (w1b_hi, w1b_lo)
                for k in range(KC):
                    need(xt_lo_done, (TILES + t) * KC + k + 1)
                    m = product(bank(("h", j)), (hi[:, f % HALF1, k, :], lo[:, f % HALF1, k, :]),
                                (xt_hi[:, k, :], xt_lo[:, k, :]), k == 0, k == KC - 1)
                m.then_inc(h_psum, 1)

            def f_(j):
                t, f = divmod(j, FC)
                need(w_lo_done, w2_chunk[f] + 1)
                need(act_lo_done, j + 1)
                for blk in range(NB):
                    if f == 0 and t:
                        need(y2_done, NB * (t - 1) + blk + 1)
                    toks = slice(blk * P, (blk + 1) * P)
                    m = product(psum[:, Y_BANK + blk, :], (act_hi[:, j % ACTS, toks], act_lo[:, j % ACTS, toks]),
                                (w2_hi[:, f, :], w2_lo[:, f, :]), f == 0, f == FC - 1)
                    if f == FC - 1 and blk < NB - 1:
                        m.then_inc(rows_psum, 1)
                m.then_inc(f_psum, 1)

            need(nan_count, 1)
            need(y_done, NB * TILES)
            run = {"xt": xt, "h": h, "f": f_}
            for kind, n in order_b:
                run[kind](n)


def kernel(x, ctx_768, L0_xattn_Wq, L0_xattn_bq, L0_xattn_Wk, L0_xattn_bk, L0_xattn_Wv, L0_xattn_bv, L0_xattn_Wo,
           L0_xattn_bo, L0_ffn_W1, L0_ffn_b1, L0_ffn_quantum_phases, L0_ffn_quantum_weights_real,
           L0_ffn_quantum_weights_imag, L0_ffn_W2, L0_ffn_b2):
    import concourse.bacc as bacc
    from concourse.bass_utils import run_bass_kernel_spmd

    def by_channel(v):
        return np.asarray(v).reshape(-1, P).T

    w1_blocks = np.asarray(L0_ffn_W1).reshape(KC, P, FC, P).transpose(2, 1, 0, 3)
    laid_out = {
        "x": x, "ctx_768": ctx_768, "wq": L0_xattn_Wq, "bq": by_channel(L0_xattn_bq), "wk": L0_xattn_Wk,
        "bk": by_channel(L0_xattn_bk), "wv": L0_xattn_Wv, "bv": L0_xattn_bv, "wo": L0_xattn_Wo,
        "bo": L0_xattn_bo, "w1": w1_blocks, "b1": by_channel(L0_ffn_b1),
        "phases": by_channel(L0_ffn_quantum_phases), "w_real": by_channel(L0_ffn_quantum_weights_real),
        "w_imag": by_channel(L0_ffn_quantum_weights_imag), "w2": L0_ffn_W2, "b2": L0_ffn_b2,
    }
    nc = bacc.Bacc("TRN2", target_bir_lowering=False, num_devices=1)
    arrays, args = {}, []
    for name, a in laid_out.items():
        a = np.ascontiguousarray(a)
        arrays[f"in_{name}"] = a
        args.append(nc.dram_tensor(f"in_{name}", a.shape, mybir.dt.from_np(a.dtype), kind="ExternalInput").ap())
    out = nc.dram_tensor("out", (B, N, C), F32, kind="ExternalOutput").ap()
    x1_dram = nc.dram_tensor("x1_dram", (B * N, C), F32, kind="Internal").ap()
    v_dram = nc.dram_tensor("v_dram", (B, KEYS, C), F32, kind="Internal").ap()
    u_dram = nc.dram_tensor("u_dram", (B, C), F32, kind="Internal").ap()
    xattn_ffn(nc, *args, out, x1_dram, v_dram, u_dram)
    r = run_bass_kernel_spmd(nc, [arrays], core_ids=[0])
    return r.results[0]["out"]
```
